# Optimizing a Trainium2 kernel written in Bass

```python
import numpy as np
import jax
import jax.numpy as jnp

def _softmax(x, axis=-1):
    return jax.nn.softmax(x, axis=axis)

def _gelu(x):
    return jax.nn.gelu(x, approximate=True)

def _silu(x):
    return jax.nn.silu(x)

def _sigmoid(x):
    return jax.nn.sigmoid(x)

def _layernorm(x, axis=-1, eps=1e-05):
    m = jnp.mean(x, axis=axis, keepdims=True)
    v = jnp.var(x, axis=axis, keepdims=True)
    return (x - m) / jnp.sqrt(v + eps)

def _scatter_add(tgt, idx, src, axis=0):
    return tgt.at[idx].add(src)

def _segment_sum(src, seg, n):
    return jax.ops.segment_sum(src, seg, n)
kernel_name = 'mk_flamingo_gated_d1_seqx_r4_59e8da'

def setup_inputs(seed: int=0):
    np.random.seed(seed)
    _w = jnp.asarray

    def _rec_inputs():
        import jax
        import jax.numpy as jnp
        _rk = jax.random.key(seed)
        x = -0.000125 + 0.9999 * jax.random.normal(jax.random.fold_in(_rk, 1), (4, 512, 512), jnp.float32)
        _lenS = 512 - jax.random.randint(jax.random.fold_in(_rk, 7), (4,), 0, max(1, 512 // 4) + 1, jnp.int32)
        _lenS2 = 512 - jax.random.randint(jax.random.fold_in(_rk, 8), (4,), 0, max(1, 512 // 4) + 1, jnp.int32)
        fside_BxS2xS2_0 = -3.05549e-07 + 0.0199987 * jax.random.normal(jax.random.fold_in(_rk, 11), (4, 512, 512), jnp.float32)
        _ctx_1024P = jax.random.normal(jax.random.fold_in(_rk, 12), (4, 16, 256), jnp.float32)
        _ctx_1024c = jax.random.dirichlet(jax.random.fold_in(_rk, 512), 0.3 * jnp.ones((16,), jnp.float32), (4, 512))
        _ctx_1024t = jnp.einsum('bsk,bkd->bsd', _ctx_1024c, _ctx_1024P)
        _ctx_1024t = _ctx_1024t * jax.lax.rsqrt(jnp.mean(jnp.square(_ctx_1024t)) + 1e-12) * 0.953939
        ctx_1024 = 6.82029e-06 + 0.0200006 * (_ctx_1024t + 0.3 * jax.random.normal(jax.random.fold_in(_rk, 612), (4, 512, 256), jnp.float32))
        _g = jax.random.normal(jax.random.fold_in(_rk, 9001), (2, 1), jnp.float32)
        _g = jnp.sign(_g) * jnp.maximum(jnp.abs(_g), 1.0) + (_g == 0) * 1.0
        g_xattn = _g[0]
        g_ffn = _g[1]
        return (x, fside_BxS2xS2_0, ctx_1024, g_xattn, g_ffn)
    x, fside_BxS2xS2_0, ctx_1024, g_xattn, g_ffn = _rec_inputs()

    def _L0_xattn_setup():
        import jax, jax.numpy as jnp
        import numpy as np
        EPS = 1e-06
        QMAX = 127.0

        def _smooth_quant_linear(x, w):
            amax_x = jnp.max(jnp.abs(x), axis=0)
            amax_w = jnp.max(jnp.abs(w), axis=0)
            s = jnp.sqrt(jnp.maximum(amax_x, EPS) / jnp.maximum(amax_w, EPS))
            s = jnp.maximum(s, EPS)
            xs = x / s
            ws = w * s
            x_scale = jnp.maximum(jnp.max(jnp.abs(xs), axis=-1, keepdims=True), EPS) / QMAX
            w_scale = jnp.maximum(jnp.max(jnp.abs(ws), axis=-1, keepdims=True), EPS) / QMAX
            x_q = jnp.clip(jnp.round(xs / x_scale), -QMAX, QMAX)
            w_q = jnp.clip(jnp.round(ws / w_scale), -QMAX, QMAX)
            return x_q @ w_q.T * x_scale * w_scale.T

        def _expert_forward(xe, guw, dw):
            h = _smooth_quant_linear(xe, guw)
            gate, up = jnp.split(h, 2, axis=-1)
            a = jax.nn.silu(gate) * up
            return _smooth_quant_linear(a, dw)
        key = jax.random.key(seed)
        k1, k2, k3 = jax.random.split(key, 3)
        E, T, D, I = (8, 512, 512, 256)
        x = jax.random.normal(k1, (E, T, D), dtype=jnp.float32)
        gate_up_weight = jax.random.normal(k2, (E, 2 * I, D), dtype=jnp.float32) * 0.02
        down_weight = jax.random.normal(k3, (E, D, I), dtype=jnp.float32) * 0.02
        return {'x': x, 'gate_up_weight': gate_up_weight, 'down_weight': down_weight}
    _L0_xattn_all = _L0_xattn_setup()
    _L0_xattn_in = {k: v for k, v in _L0_xattn_all.items() if k in ()}
    del _L0_xattn_all

    def _L0_ffn_setup():
        import jax, jax.numpy as jnp
        import numpy as np
        H = 512
        I = 352
        E = 16
        K = 2
        N_SHARED = 2
        IS = I * N_SHARED
        ROUTED_SCALE = 1.0
        CAPACITY = 256

        def _moe_forward(hidden_states, gate_w, w_gate, w_up, w_down, ws_gate, ws_up, ws_down):
            B, S, _ = hidden_states.shape
            x = hidden_states.reshape(-1, H)
            T = x.shape[0]
            logits = jnp.einsum('th,eh->te', x.astype(jnp.float32), gate_w.astype(jnp.float32))
            scores = jax.nn.softmax(logits, axis=-1)
            topk_w, topk_idx = jax.lax.top_k(scores, K)
            topk_w = (topk_w * ROUTED_SCALE).astype(x.dtype)
            flat_idx = topk_idx.reshape(-1)
            order = jnp.argsort(flat_idx)
            sorted_e = flat_idx[order]
            sorted_t = order // K
            counts = jnp.bincount(flat_idx, length=E)
            starts = jnp.cumsum(counts) - counts
            pos = jnp.arange(T * K) - starts[sorted_e]
            buf = jnp.zeros((E, CAPACITY, H), x.dtype).at[sorted_e, pos].set(x[sorted_t], mode='drop')
            g = jax.nn.silu(jnp.einsum('ech,ehi->eci', buf, w_gate))
            u = jnp.einsum('ech,ehi->eci', buf, w_up)
            expert_out = jnp.einsum('eci,eih->ech', g * u, w_down)
            gathered = expert_out[sorted_e, pos]
            out_flat = jnp.zeros((T * K, H), x.dtype).at[order].set(gathered)
            y = (out_flat.reshape(T, K, H) * topk_w[..., None]).sum(axis=1)
            sh = jnp.einsum('ti,ih->th', jax.nn.silu(x @ ws_gate) * (x @ ws_up), ws_down)
            return (y + sh).reshape(B, S, H)
        key = jax.random.key(seed)
        ks = jax.random.split(key, 8)
        B, S = (2, 256)
        scale = 0.02
        return {'hidden_states': jax.random.normal(ks[0], (B, S, H), jnp.float32), 'gate_w': jax.random.normal(ks[1], (E, H), jnp.float32) * scale, 'w_gate': jax.random.normal(ks[2], (E, H, I), jnp.float32) * scale, 'w_up': jax.random.normal(ks[3], (E, H, I), jnp.float32) * scale, 'w_down': jax.random.normal(ks[4], (E, I, H), jnp.float32) * scale, 'ws_gate': jax.random.normal(ks[5], (H, IS), jnp.float32) * scale, 'ws_up': jax.random.normal(ks[6], (H, IS), jnp.float32) * scale, 'ws_down': jax.random.normal(ks[7], (IS, H), jnp.float32) * scale}
    _L0_ffn_all = _L0_ffn_setup()
    _L0_ffn_in = {k: v for k, v in _L0_ffn_all.items() if k in ('gate_w', 'w_gate', 'w_up', 'w_down', 'ws_gate', 'ws_up', 'ws_down')}
    del _L0_ffn_all
    return {'x': x, 'fside_BxS2xS2_0': fside_BxS2xS2_0, 'ctx_1024': ctx_1024, 'g_xattn': g_xattn, 'g_ffn': g_ffn, 'L0_ffn_gate_w': _L0_ffn_in['gate_w'], 'L0_ffn_w_gate': _L0_ffn_in['w_gate'], 'L0_ffn_w_up': _L0_ffn_in['w_up'], 'L0_ffn_w_down': _L0_ffn_in['w_down'], 'L0_ffn_ws_gate': _L0_ffn_in['ws_gate'], 'L0_ffn_ws_up': _L0_ffn_in['ws_up'], 'L0_ffn_ws_down': _L0_ffn_in['ws_down']}

def reference(x, fside_BxS2xS2_0, ctx_1024, g_xattn, g_ffn, L0_ffn_gate_w, L0_ffn_w_gate, L0_ffn_w_up, L0_ffn_w_down, L0_ffn_ws_gate, L0_ffn_ws_up, L0_ffn_ws_down):
    import jax
    import jax.numpy as jnp

    def _L0_xattn_ref(x, gate_up_weight, down_weight):
        import jax, jax.numpy as jnp
        import numpy as np
        EPS = 1e-06
        QMAX = 127.0

        def _smooth_quant_linear(x, w):
            amax_x = jnp.max(jnp.abs(x), axis=0)
            amax_w = jnp.max(jnp.abs(w), axis=0)
            s = jnp.sqrt(jnp.maximum(amax_x, EPS) / jnp.maximum(amax_w, EPS))
            s = jnp.maximum(s, EPS)
            xs = x / s
            ws = w * s
            x_scale = jnp.maximum(jnp.max(jnp.abs(xs), axis=-1, keepdims=True), EPS) / QMAX
            w_scale = jnp.maximum(jnp.max(jnp.abs(ws), axis=-1, keepdims=True), EPS) / QMAX
            x_q = jnp.clip(jnp.round(xs / x_scale), -QMAX, QMAX)
            w_q = jnp.clip(jnp.round(ws / w_scale), -QMAX, QMAX)
            return x_q @ w_q.T * x_scale * w_scale.T

        def _expert_forward(xe, guw, dw):
            h = _smooth_quant_linear(xe, guw)
            gate, up = jnp.split(h, 2, axis=-1)
            a = jax.nn.silu(gate) * up
            return _smooth_quant_linear(a, dw)
        return jax.vmap(_expert_forward)(x, gate_up_weight, down_weight)

    def _L0_ffn_ref(hidden_states, gate_w, w_gate, w_up, w_down, ws_gate, ws_up, ws_down):
        import jax, jax.numpy as jnp
        import numpy as np
        H = 512
        I = 352
        E = 16
        K = 2
        N_SHARED = 2
        IS = I * N_SHARED
        ROUTED_SCALE = 1.0
        CAPACITY = 256

        def _moe_forward(hidden_states, gate_w, w_gate, w_up, w_down, ws_gate, ws_up, ws_down):
            B, S, _ = hidden_states.shape
            x = hidden_states.reshape(-1, H)
            T = x.shape[0]
            logits = jnp.einsum('th,eh->te', x.astype(jnp.float32), gate_w.astype(jnp.float32))
            scores = jax.nn.softmax(logits, axis=-1)
            topk_w, topk_idx = jax.lax.top_k(scores, K)
            topk_w = (topk_w * ROUTED_SCALE).astype(x.dtype)
            flat_idx = topk_idx.reshape(-1)
            order = jnp.argsort(flat_idx)
            sorted_e = flat_idx[order]
            sorted_t = order // K
            counts = jnp.bincount(flat_idx, length=E)
            starts = jnp.cumsum(counts) - counts
            pos = jnp.arange(T * K) - starts[sorted_e]
            buf = jnp.zeros((E, CAPACITY, H), x.dtype).at[sorted_e, pos].set(x[sorted_t], mode='drop')
            g = jax.nn.silu(jnp.einsum('ech,ehi->eci', buf, w_gate))
            u = jnp.einsum('ech,ehi->eci', buf, w_up)
            expert_out = jnp.einsum('eci,eih->ech', g * u, w_down)
            gathered = expert_out[sorted_e, pos]
            out_flat = jnp.zeros((T * K, H), x.dtype).at[order].set(gathered)
            y = (out_flat.reshape(T, K, H) * topk_w[..., None]).sum(axis=1)
            sh = jnp.einsum('ti,ih->th', jax.nn.silu(x @ ws_gate) * (x @ ws_up), ws_down)
            return (y + sh).reshape(B, S, H)
        return _moe_forward(hidden_states, gate_w, w_gate, w_up, w_down, ws_gate, ws_up, ws_down)
    x = x + jnp.tanh(g_xattn[0]) * _L0_xattn_ref(_layernorm(x, axis=-1), fside_BxS2xS2_0, ctx_1024)
    x = x + jnp.tanh(g_ffn[0]) * _L0_ffn_ref(_layernorm(x, axis=-1), L0_ffn_gate_w, L0_ffn_w_gate, L0_ffn_w_up, L0_ffn_w_down, L0_ffn_ws_gate, L0_ffn_ws_up, L0_ffn_ws_down)
    return x

_drawn_inputs = setup_inputs


def setup_inputs(seed=0):
    import zlib

    import numpy as np

    out = dict(_drawn_inputs(seed))
    spreads = {}
    factors = {'L0_ffn_gate_w': 8.0,
     'L0_ffn_w_gate': 8.0,
     'L0_ffn_w_up': 7.842,
     'L0_ffn_w_down': 7.777,
     'L0_ffn_ws_gate': 8.0,
     'L0_ffn_ws_up': 8.0,
     'L0_ffn_ws_down': 8.0}
    for name, (base, spread) in spreads.items():
        noise = np.random.default_rng([zlib.crc32(name.encode()), seed]).standard_normal(out[name].shape)
        drawn = base * np.exp(spread * noise) if base else spread * noise
        out[name] = jnp.asarray(drawn.astype(out[name].dtype))
    for name, factor in factors.items():
        out[name] = (out[name] * factor).astype(out[name].dtype)
    return out
```

```python
from contextlib import ExitStack

import concourse.bass as bass
from concourse import mybir

ALU = mybir.AluOpType
ACT = mybir.ActivationFunctionType
AX = mybir.AxisListType
F32 = mybir.dt.float32
R32 = mybir.dt.float32r
BF16 = mybir.dt.bfloat16
U32 = mybir.dt.uint32

P = 128
BANK = 512
LN_EPS = 1e-5
Q_EPS = 1e-6
QMAX = 127.0
MAGIC = 12582912.0
EXP_MIN = -87.33654


def flamingo_block(nc, x, guw, dw, g_x, g_f, gate_w, w_gate, w_up, w_down, s_gate, s_up, s_down, out):
    B, T, D = x.shape
    I2 = dw.shape[2]
    E, _, I = w_gate.shape
    IS = s_gate.shape[1]
    CAP = 256
    HALF = CAP // P
    J = T // P
    C = D // P
    C2 = I2 // P
    NT = B * J
    M = -(-I // P)
    ROWS = [min(P, I - m * P) for m in range(M)]
    MFULL = IS // P
    SREST = IS - MFULL * P
    MS = MFULL + 1
    GU = 2 * IS
    assert T == BANK and D == BANK and 2 * SREST == P and 2 * I2 == D and HALF == 2 and M == 3 and E % 2 == 0

    x_v = x.rearrange("b (p j) d -> b p j d", j=J)
    out_v = out.rearrange("b (p j) d -> b p j d", j=J)
    guw_v = guw.rearrange("b (j p) d -> b p j d", p=P)
    dw_v = dw.rearrange("b (j p) d -> b p j d", p=P)
    wg_v = w_gate.rearrange("e (c p) i -> e p c i", p=P)
    wu_v = w_up.rearrange("e (c p) i -> e p c i", p=P)
    sg_v = s_gate.rearrange("(c p) i -> p c i", p=P)
    su_v = s_up.rearrange("(c p) i -> p c i", p=P)

    x2n_dram = nc.dram_tensor("x2n_scratch", (B * T, D), F32).ap()
    eo_dram = nc.dram_tensor("expert_out_scratch", (E * CAP, D), F32).ap()
    x2n_v = x2n_dram.rearrange("(b p j) d -> b p j d", p=P, j=J)
    eo_v = eo_dram.rearrange("(e h p) d -> e p h d", h=HALF, p=P)

    base = -(-nc.sbuf_base // 32) * 32

    def place(cursor, name, shape, dt=F32):
        n = 2 if dt == BF16 else 4
        for k in shape[1:]:
            n *= k
        at = cursor[0]
        cursor[0] += -(-n // 32) * 32
        return nc.alloc_sbuf_tensor_at(name, shape, dt, offset=at)

    cur = [base]
    x2 = place(cur, "x2", [P, B, J, D])
    ident = place(cur, "ident", [P, P])
    ones = place(cur, "ones", [P, P])
    before = place(cur, "before", [P, P])
    slot_no = place(cur, "slot_no", [P, CAP])
    rev_e = place(cur, "rev_e", [P, E])
    tok_no = place(cur, "tok_no", [P, NT])
    powers = place(cur, "powers", [P, 2, J])
    ln_eps = place(cur, "ln_eps", [P, J])
    after_wait = place(cur, "after_wait", [P, 1])
    tg = place(cur, "tg", [P, 2])
    lg = place(cur, "lg", [P, NT, E])
    gate_hi = place(cur, "gate_hi", [P, C, E], R32)
    gate_lo = place(cur, "gate_lo", [P, C, E], R32)
    wts = place(cur, "wts", [P, 2, NT])
    slots = place(cur, "slots", [P, 2, NT], U32)
    slot_col = place(cur, "slot_col", [P, 2, J, 2], U32)
    idx = place(cur, "idx", [P, HALF, E], U32)
    idx_col = place(cur, "idx_col", [P, 2, HALF], U32)

    region = cur[0]
    w1 = place(cur, "w1", [P, J, D])
    xn = place(cur, "xn", [P, J, D])
    xs = place(cur, "xs", [P, J, D])
    q_x = place(cur, "q_x", [P, C, T], BF16)
    q_w = place(cur, "q_w", [P, C, D], BF16)
    q_x2 = place(cur, "q_x2", [P, C2, T], BF16)
    q_w2 = place(cur, "q_w2", [P, C2, D], BF16)
    diag = place(cur, "diag", [P, BANK])
    row_s = place(cur, "row_s", [P, D])
    row_w = place(cur, "row_w", [P, D])
    bn = place(cur, "bn", [P, J, 6])
    mv = place(cur, "mv", [P, J, 2])
    small = {n: place(cur, n, [P, J]) for n in (
        "var_eps", "rstd", "amax_w", "amax_x", "recip_w", "ratio", "root", "smooth", "rsmooth",
        "x_max", "w_max", "x_step", "x_inv", "w_step", "w_inv")}
    gate_row = place(cur, "gate_row", [E, D])
    route = cur[0]
    ws = place(cur, "ws", [P, J, D])
    w2 = place(cur, "w2", [P, J, I2])
    gated = place(cur, "gated", [P, J, I2])
    shared = cur[0]
    xt_hi = place(cur, "xt_hi", [P, C, T], R32)
    xt_lo = place(cur, "xt_lo", [P, C, T], R32)
    sw_hi = place(cur, "sw_hi", [P, C, GU], R32)
    sw_lo = place(cur, "sw_lo", [P, C, GU], R32)
    sd_hi = place(cur, "sd_hi", [P, MS, D], R32)
    sd_lo = place(cur, "sd_lo", [P, MS, D], R32)
    sh_hhi = place(cur, "sh_hhi", [P, 3, T], R32)
    sh_hlo = place(cur, "sh_hlo", [P, 3, T], R32)
    sh_silu = place(cur, "sh_silu", [P, 2, T])
    sh_hid = place(cur, "sh_hid", [P, 2, T])
    sh_rest = place(cur, "sh_rest", [SREST, T])

    cur = [route]
    r_key = place(cur, "r_key", [P, NT, E])
    r_exp = place(cur, "r_exp", [P, NT, E])
    r_oh = [place(cur, f"r_oh{k}", [P, NT, E]) for k in range(2)]
    r_tmp = place(cur, "r_tmp", [P, NT, E])
    r_cnt = place(cur, "r_cnt", [P, NT, E])
    r_rank = place(cur, "r_rank", [P, NT, E])
    r_tok = [place(cur, f"r_tok{k}", [P, NT, E]) for k in range(2)]
    r_seq = place(cur, "r_seq", [P, 2, B, E])
    r_top = place(cur, "r_top", [P, 12, NT])
    pos_oh = place(cur, "pos_oh", [P, 4, CAP])
    assert cur[0] <= shared

    cur = [region]
    raw_gu, raw_d, w_hi, w_lo, wd_hi, wd_lo, ex_xhi, ex_xlo, eo, xg = ([None, None] for _ in range(10))
    raw_gu[0] = place(cur, "raw_gu0", [P, 2, C, I])
    raw_d[0] = place(cur, "raw_d0", [P, M, D])
    w_hi[0] = place(cur, "w_hi0", [P, 2, C, I], R32)
    w_lo[0] = place(cur, "w_lo0", [P, 2, C, I], R32)
    xg[0] = place(cur, "xg0", [P, HALF, D])
    assert cur[0] <= route
    cur = [route]
    xg[1] = place(cur, "xg1", [P, HALF, D])
    wd_hi[0] = place(cur, "wd_hi0", [P, M, D], R32)
    wd_lo[0] = place(cur, "wd_lo0", [P, M, D], R32)
    assert cur[0] <= shared
    cur = [shared]
    raw_gu[1] = place(cur, "raw_gu1", [P, 2, C, I])
    raw_d[1] = place(cur, "raw_d1", [P, M, D])
    w_hi[1] = place(cur, "w_hi1", [P, 2, C, I], R32)
    w_lo[1] = place(cur, "w_lo1", [P, 2, C, I], R32)
    wd_hi[1] = place(cur, "wd_hi1", [P, M, D], R32)
    wd_lo[1] = place(cur, "wd_lo1", [P, M, D], R32)
    for q in range(2):
        ex_xhi[q] = place(cur, f"ex_xhi{q}", [P, C, CAP], R32)
        ex_xlo[q] = place(cur, f"ex_xlo{q}", [P, C, CAP], R32)
        eo[q] = place(cur, f"eo{q}", [P, HALF, D])
    ex_hhi = place(cur, "ex_hhi", [P, M, CAP], R32)
    ex_hlo = place(cur, "ex_hlo", [P, M, CAP], R32)
    ex_silu = place(cur, "ex_silu", [P, 2, CAP])
    ex_hid = place(cur, "ex_hid", [P, 2, CAP])
    cur = [region]
    got = place(cur, "got", [P, 2, J, 2, D])

    stage_gu = x2[:, 1:4].rearrange("p b j d -> p (b j d)")[:, 0:C * GU].rearrange("p (c n) -> p c n", c=C)
    stage_d = x2[:, 1:4].rearrange("p b j d -> p (b j d)")[:, 0:MS * D].rearrange("p (m n) -> p m n", m=MS)

    U_WT, U_XT, U_S, U_RS, U_QX, U_QW, U_WSTEP, U_H = 0, 4, 8, 9, 10, 14, 18, 19
    U_W2T, U_AT, U_S2, U_QA, U_QW2, U_W2STEP, U_Y, U_X2T, U_LG, UNITS = 23, 25, 27, 28, 30, 32, 33, 37, 41, 42
    LINKS = 20
    RING = 3

    with ExitStack() as ctx:
        def sem(name):
            return ctx.enter_context(nc.semaphore(name))

        ps_a = ctx.enter_context(nc.psum_tensor("ps_a", [P, 2, BANK], F32))
        ps_gu = ctx.enter_context(nc.psum_tensor("ps_gu", [P, 2, BANK], F32))
        ps_d = ctx.enter_context(nc.psum_tensor("ps_d", [P, 4, BANK], F32))
        ps_xt = ps_a[:, :, :].rearrange("p u (c n) -> p (u c) n", n=CAP)

        x_in, w1_in, w2_in, gates_in, router_in = (sem(n) for n in ("x_in", "w1_in", "w2_in", "gates_in", "router_in"))
        sgu_in, sd_in = sem("sgu_in"), sem("sd_in")
        x2n_out = sem("x2n_out")
        const_ready, masks_ready, tanh_done = sem("const_ready"), sem("masks_ready"), sem("tanh_done")
        router_t, router_hi, router_lo = sem("router_t"), sem("router_hi"), sem("router_lo")
        sgu_hi, sgu_lo, sdn_hi, sdn_lo = sem("sgu_hi"), sem("sgu_lo"), sem("sdn_hi"), sem("sdn_lo")
        unit_full = sem("unit_full")
        unit_free = [sem("unit_free0"), sem("unit_free1")]
        chain = sem("chain")
        var_done, rstd_done, root_done = sem("var_done"), sem("rstd_done"), sem("root_done")
        ratio_done, smooth_diag, step_diag = sem("ratio_done"), sem("smooth_diag"), sem("step_diag")
        xn_done, ws_done = sem("xn_done"), sem("ws_done")
        x_steps, w_steps = sem("x_steps"), sem("w_steps")
        qx_done, qw_done = sem("qx_done"), sem("qw_done")
        silu_done, gated_done = sem("silu_done"), sem("gated_done")
        x2n_done, xt_hi_done = sem("x2n_done"), sem("xt_hi_done")
        sh_gu, sh_sg, sh_h, sh_hi, sh_lo, sh_ring, sh_sum = (
            sem(n) for n in ("sh_gu", "sh_sg", "sh_h", "sh_hi", "sh_lo", "sh_ring", "sh_sum"))
        rt_key = sem("rt_key")
        rt, r_exp_done, seq_done, rank_done = sem("rt"), sem("r_exp_done"), sem("seq_done"), sem("rank_done")
        pos_done, table_mm, idx_ready, routed = (
            sem("pos_done"), sem("table_mm"), sem("idx_ready"), sem("routed"))
        raw_in = [sem("raw_in0"), sem("raw_in1")]
        xg_in = [sem("xg_in0"), sem("xg_in1")]
        eo_out = [sem("eo_out0"), sem("eo_out1")]
        col_done, ex_xt, ex_xh, ex_x = sem("col_done"), sem("ex_xt"), sem("ex_xh"), sem("ex_x")
        ex_whi, ex_wlo, ex_wdhi, ex_wdlo = sem("ex_whi"), sem("ex_wlo"), sem("ex_wdhi"), sem("ex_wdlo")
        ex_gu, ex_sg, ex_h, ex_hi, ex_lo, ex_d, ex_eo = (
            sem(n) for n in ("ex_gu", "ex_sg", "ex_h", "ex_hi", "ex_lo", "ex_d", "ex_eo"))
        cols_staged = sem("cols_staged")
        slot_cols, got_in, sum_half, summed, out_done = (
            sem("slot_cols"), [sem("got_in0"), sem("got_in1")], sem("sum_half"), sem("summed"), sem("out_done"))

        block = ctx.enter_context(nc.Block())

        def bank(u):
            return ps_a[:, u % 2, :]

        def filled(b, u):
            return UNITS * b + u + 1

        def read(b, u):
            return UNITS // 2 * b + u // 2 + 1

        @block.sync
        def _(sp):
            def load_w1(b):
                sp.dma_start(w1[:], guw_v[b]).then_inc(w1_in, 16)

            def load_w2(b):
                sp.dma_start(w2[:], dw_v[b]).then_inc(w2_in, 16)

            def load_raw(e, q):
                sp.dma_start(raw_gu[q][:, 0], wg_v[e]).then_inc(raw_in[q], 16)
                sp.dma_start(raw_gu[q][:, 1], wu_v[e]).then_inc(raw_in[q], 16)
                sp.dma_start(raw_d[q][:, 0:M - 1, :],
                             w_down[e, 0:(M - 1) * P, :].rearrange("(m p) d -> p m d", p=P)).then_inc(raw_in[q], 16)
                sp.dma_start(raw_d[q][0:ROWS[M - 1], M - 1, :], w_down[e, (M - 1) * P:I, :]).then_inc(raw_in[q], 16)

            def store_x2n(b):
                sp.wait_ge(x2n_done, b + 1)
                sp.dma_start(x2n_v[b], xs[:]).then_inc(x2n_out, 16)

            def store_eo(e, q):
                sp.wait_ge(ex_eo, e + 1)
                sp.dma_start(eo_v[e], eo[q][:]).then_inc(eo_out[q], 16)

            sp.dma_start(x2[:, 0], x_v[0]).then_inc(x_in, 16)
            load_w1(0)
            sp.dma_start(gate_row[:], gate_w).then_inc(router_in, 16)
            sp.dma_start(tg[:, 0:1], g_x.rearrange("(a n) -> a n", a=1).broadcast_to((P, 1))).then_inc(gates_in, 16)
            sp.dma_start(tg[:, 1:2], g_f.rearrange("(a n) -> a n", a=1).broadcast_to((P, 1))).then_inc(gates_in, 16)
            load_w2(0)
            full, rest = slice(0, MFULL * P), slice(MFULL * P, IS)
            for n, (src, part, at) in enumerate(((sg_v, full, 0), (su_v, full, MFULL * P),
                                                 (sg_v, rest, 2 * MFULL * P), (su_v, rest, 2 * MFULL * P + SREST))):
                width = part.stop - part.start
                sp.dma_start(stage_gu[:, :, at:at + width], src[:, :, part]).then_inc(sgu_in, 16)
            sp.wait_ge(sgu_hi, 1)
            sp.wait_ge(sgu_lo, 2)
            sp.dma_start(stage_d[:, 0:MFULL, :],
                         s_down[0:MFULL * P, :].rearrange("(m p) d -> p m d", p=P)).then_inc(sd_in, 16)
            sp.dma_start(stage_d[0:SREST, MFULL, :], s_down[MFULL * P:IS, :]).then_inc(sd_in, 16)
            sp.wait_ge(sdn_hi, 1)
            sp.wait_ge(sdn_lo, 1)
            sp.dma_start(x2[:, 1:B], x_v[1:B].rearrange("b p j d -> p b j d")).then_inc(x_in, 16)
            with sp.Fori(1, B) as b:
                sp.wait_ge(ws_done, 2 * b - 1)
                load_w1(b)
                sp.wait_ge(ws_done, 2 * b)
                load_w2(b)
                store_x2n(b - 1)
            store_x2n(B - 1)

            sp.wait_ge(unit_free[U_LG % 2], read(B - 1, U_LG))
            sp.wait_ge(x2n_out, 16 * B)
            load_raw(0, 0)
            sp.wait_ge(sh_sum, B)
            load_raw(1, 1)

            def step(e, q):
                sp.wait_ge(ex_whi, e + 1)
                sp.wait_ge(ex_wlo, e + 1)
                sp.wait_ge(ex_wdhi, e + 1)
                sp.wait_ge(ex_wdlo, e + 1)
                load_raw(e + 2, q)

            step(0, 0)
            with sp.Fori(0, E // 2 - 2) as r:
                step(2 * r + 1, 1)
                store_eo(2 * r, 0)
                step(2 * r + 2, 0)
                store_eo(2 * r + 1, 1)
            step(E - 3, 1)
            for e in range(E - 4, E):
                store_eo(e, e % 2)
            sp.wait_ge(eo_out[0], 16 * (E // 2))
            sp.wait_ge(eo_out[1], 16 * (E // 2))
            with sp.Fori(0, B) as b:
                sp.wait_ge(summed, b + 1)
                sp.dma_start(out_v[b], x2[:, b]).then_inc(out_done, 16)
            sp.wait_ge(out_done, 16 * B)

        @block.gpsimd
        def _(pool):
            pool.memset(ident[:], 0.0).then_inc(const_ready, 1)
            pool.memset(ones[:], 1.0).then_inc(const_ready, 1)
            pool.memset(powers[:, 0, :], 0.5).then_inc(const_ready, 1)
            pool.memset(powers[:, 1, :], -0.5).then_inc(const_ready, 1)
            pool.memset(ln_eps[:], LN_EPS).then_inc(const_ready, 1)
            pool.iota(slot_no[:], [[1, CAP]], base=0, channel_multiplier=0,
                      allow_small_or_imprecise_dtypes=True).then_inc(const_ready, 1)
            pool.iota(rev_e[:], [[-1, E]], base=E, channel_multiplier=0,
                      allow_small_or_imprecise_dtypes=True).then_inc(const_ready, 1)
            pool.iota(tok_no[:], [[T, B], [1, J]], base=0, channel_multiplier=J,
                      allow_small_or_imprecise_dtypes=True).then_inc(const_ready, 1)
            pool.wait_ge(const_ready, 8)
            pool.affine_select(out=ident[:], in_=ident[:], compare_op=ALU.not_equal, fill=1.0, base=0,
                               pattern=[[-1, P]], channel_multiplier=1).then_inc(masks_ready, 1)
            pool.affine_select(out=before[:], in_=ones[:], compare_op=ALU.is_gt, fill=0.0, base=0,
                               pattern=[[1, P]], channel_multiplier=-1).then_inc(masks_ready, 1)

            def norm_scale(n):
                pool.wait_ge(var_done, n + 1)
                pool.tensor_tensor(small["var_eps"][:], mv[:, :, 1], ln_eps[:], ALU.add).then_inc(rstd_done, 1)
                pool.wait_ge(rstd_done, 2 * n + 1)
                pool.tensor_tensor(small["rstd"][:], small["var_eps"][:], powers[:, 1, :], ALU.pow).then_inc(rstd_done, 1)

            def root(n, width):
                pool.wait_ge(ratio_done, n + 1)
                pool.tensor_tensor(small["root"][:, 0:width], small["ratio"][:, 0:width], powers[:, 0, 0:width],
                                   ALU.pow).then_inc(root_done, 1)

            def smooth_w1(b):
                pool.wait_ge(unit_free[U_S % 2], read(b, U_S))
                pool.wait_ge(w1_in, 16 * b + 16)
                pool.tensor_tensor(ws[:], w1[:], row_s[:].unsqueeze(1).broadcast_to((P, J, D)),
                                   ALU.mult).then_inc(ws_done, 1)

            def smooth_w2(b):
                pool.wait_ge(unit_free[U_S2 % 2], read(b, U_S2))
                pool.wait_ge(w2_in, 16 * b + 16)
                pool.tensor_tensor(ws[:, :, 0:I2], w2[:], row_s[:, 0:I2].unsqueeze(1).broadcast_to((P, J, I2)),
                                   ALU.mult).then_inc(ws_done, 1)

            def split_shared(c0, c1):
                pool.wait_ge(sgu_hi, 1)
                pool.tensor_tensor(sw_lo[:, c0:c1, :], stage_gu[:, c0:c1, :], sw_hi[:, c0:c1, :].bitcast(F32),
                                   ALU.subtract).then_inc(sgu_lo, 1)

            norm_scale(0)
            split_shared(0, C // 2)
            root(0, C)
            smooth_w1(0)
            split_shared(C // 2, C)
            root(1, C2)
            smooth_w2(0)
            pool.wait_ge(sdn_hi, 1)
            pool.tensor_tensor(sd_lo[:, 0:MFULL, :], stage_d[:, 0:MFULL, :], sd_hi[:, 0:MFULL, :].bitcast(F32), ALU.subtract)
            pool.tensor_tensor(sd_lo[0:SREST, MFULL, :], stage_d[0:SREST, MFULL, :], sd_hi[0:SREST, MFULL, :].bitcast(F32),
                               ALU.subtract).then_inc(sdn_lo, 1)
            norm_scale(1)
            with pool.Fori(1, B) as b:
                norm_scale(2 * b)
                root(2 * b, C)
                smooth_w1(b)
                root(2 * b + 1, C2)
                smooth_w2(b)
                norm_scale(2 * b + 1)

            def gather(e, q):
                pool.tensor_copy(idx_col[:, q, :], idx[:, :, e]).then_inc(col_done, 1)
                pool.wait_ge(col_done, e + 1)
                pool.sem_inc(cols_staged, 1)
                for h in range(HALF):
                    pool.indirect_dma_start(xg[q][:, h, :], None, x2n_dram,
                                            bass.IndirectOffsetOnAxis(idx_col[:, q, h:h + 1], 0)).then_inc(xg_in[q], 16)

            def split(e, q):
                pool.wait_ge(ex_whi, e + 1)
                pool.tensor_tensor(w_lo[q][:], raw_gu[q][:], w_hi[q][:].bitcast(F32), ALU.subtract).then_inc(ex_wlo, 1)

            pool.wait_ge(x2n_out, 16 * B)
            split(0, 0)
            pool.wait_ge(idx_ready, 1)
            pool.wait_ge(routed, 1)
            gather(0, 0)
            gather(1, 1)

            def step(e, q):
                pool.wait_ge(ex_xt, e + 1)
                gather(e + 2, q)
                split(e + 1, 1 - q)

            step(0, 0)
            with pool.Fori(0, E // 2 - 2) as r:
                step(2 * r + 1, 1)
                step(2 * r + 2, 0)
            step(E - 3, 1)
            split(E - 1, 1)

            pool.wait_ge(eo_out[0], 16 * (E // 2))
            pool.wait_ge(eo_out[1], 16 * (E // 2))

            def gather_rows(b, k):
                pool.tensor_copy(slot_col[:, k].rearrange("p j n -> p n j"),
                                 slots[:].rearrange("p n (b j) -> p b n j", j=J)[:, b]).then_inc(slot_cols, 1)
                pool.wait_ge(slot_cols, b + 1)
                pool.sem_inc(cols_staged, 1)
                for j in range(J):
                    for n in range(2):
                        pool.indirect_dma_start(got[:, k, j, n, :], None, eo_dram,
                                                bass.IndirectOffsetOnAxis(slot_col[:, k, j, n:n + 1], 0)).then_inc(got_in[k], 16)

            gather_rows(0, 0)
            gather_rows(1, 1)
            with pool.Fori(1, B // 2) as r:
                for k in range(2):
                    pool.wait_ge(summed, 2 * r + k - 1)
                    gather_rows(2 * r + k, k)

        @block.scalar
        def _(act):
            act.wait_ge(gates_in, 32)
            act.activation(tg[:], tg[:], ACT.Tanh).then_inc(tanh_done, 1)
            act.wait_ge(router_t, 1)
            act.activation(gate_hi[:], ps_gu[:, 0, 0:C * E].rearrange("p (c e) -> p c e", c=C),
                           ACT.Copy).then_inc(router_hi, 1)
            act.wait_ge(sgu_in, 64)
            act.activation(sw_hi[:], stage_gu, ACT.Copy).then_inc(sgu_hi, 1)

            def copy_row(b, u, dst, scale=1.0):
                act.wait_ge(unit_full, filled(b, u))
                act.activation(dst, bank(u), ACT.Copy, scale=scale).then_inc(unit_free[u % 2], 1)

            def quantise(b, n, src, width, inv, steps, done):
                act.wait_ge(steps, 2 * b + n + 1)
                for j in range(J):
                    last = act.activation(src[:, j, 0:width], src[:, j, 0:width], ACT.Copy, bias=MAGIC,
                                          scale=small[inv][:, j:j + 1])
                last.then_inc(done, 1)

            def integers(b, u0, n, dst):
                for c in range(n):
                    act.wait_ge(unit_full, filled(b, u0 + c))
                    act.activation(dst[:, c, :], bank(u0 + c), ACT.Copy, bias=-MAGIC).then_inc(unit_free[(u0 + c) % 2], 1)

            def layer_silu(b):
                act.wait_ge(unit_free[(U_H + J - 1) % 2], read(b, U_H + J - 1))
                act.activation(gated[:], xn[:, :, 0:I2], ACT.Silu).then_inc(silu_done, 1)

            def x_hi(b):
                for c in range(C):
                    act.wait_ge(unit_full, filled(b, U_X2T + c))
                    act.activation(xt_hi[:, c, :], bank(U_X2T + c), ACT.Copy).then_inc(xt_hi_done, 1)

            def logits(b):
                act.wait_ge(unit_full, filled(b, U_LG))
                act.activation(lg[:].rearrange("p (b j) e -> p b (j e)", j=J)[:, b], bank(U_LG)[:, 0:J * E],
                               ACT.Copy).then_inc(unit_free[U_LG % 2], 1)

            def sh(f, m):
                n = MS * f + m
                k = P if m < MFULL else SREST
                act.wait_ge(sh_gu, n + 1)
                if m == MFULL:
                    act.activation(sh_rest[:], ps_gu[SREST:P, 0, :], ACT.Copy)
                act.activation(sh_silu[0:k, m % 2, :], ps_gu[0:k, 0, :], ACT.Silu).then_inc(sh_sg, 1)
                act.wait_ge(sh_h, n + 1)
                act.wait_ge(sh_ring, n + 1)
                act.activation(sh_hhi[0:k, m % RING, :], sh_hid[0:k, m % 2, :], ACT.Copy).then_inc(sh_hi, 1)

            def split_down():
                act.wait_ge(sd_in, 32)
                act.activation(sd_hi[:, 0:MFULL, :], stage_d[:, 0:MFULL, :], ACT.Copy)
                act.activation(sd_hi[0:SREST, MFULL, :], stage_d[0:SREST, MFULL, :], ACT.Copy).then_inc(sdn_hi, 1)

            def sequence(b, f):
                def sh_chunk(m):
                    if f is not None:
                        sh(f, m)

                sh_chunk(0)
                copy_row(b, U_S, row_s[:])
                sh_chunk(1)
                quantise(b, 0, xs, D, "x_inv", x_steps, qx_done)
                quantise(b, 0, ws, D, "w_inv", w_steps, qw_done)
                integers(b, U_QX, C, q_x)
                integers(b, U_QW, C, q_w)
                copy_row(b, U_WSTEP, row_w[:])
                sh_chunk(2)
                layer_silu(b)
                sh_chunk(3)
                sh_chunk(4)
                copy_row(b, U_S2, row_s[:])
                quantise(b, 1, xs, I2, "x_inv", x_steps, qx_done)
                quantise(b, 1, ws, I2, "w_inv", w_steps, qw_done)
                if f is None:
                    split_down()
                sh_chunk(5)
                integers(b, U_QA, C2, q_x2)
                integers(b, U_QW2, C2, q_w2)
                copy_row(b, U_W2STEP, row_w[:], scale=tg[:, 0:1])
                x_hi(b)
                logits(b)

            act.wait_ge(tanh_done, 1)
            sequence(0, None)
            with act.Fori(1, B) as b:
                sequence(b, b - 1)

            def weights_gu(e, k, q):
                act.wait_ge(raw_in[q], 64 * k + 64)
                act.activation(w_hi[q][:], raw_gu[q][:], ACT.Copy).then_inc(ex_whi, 1)

            def weights_d(e, q):
                act.activation(wd_hi[q][:, 0:M - 1, :], raw_d[q][:, 0:M - 1, :], ACT.Copy)
                act.activation(wd_hi[q][0:ROWS[M - 1], M - 1, :], raw_d[q][0:ROWS[M - 1], M - 1, :],
                               ACT.Copy).then_inc(ex_wdhi, 1)

            def tokens(e, q):
                act.wait_ge(ex_xt, e + 1)
                act.activation(ex_xhi[q][:], ps_xt, ACT.Copy).then_inc(ex_xh, 1)

            def hidden(e, q, m, first):
                n, k = M * e + m, ROWS[m]
                act.wait_ge(ex_gu, n + 1)
                act.activation(ex_silu[0:k, (q + m) % 2, :], ps_gu[0:k, (q + m) % 2, 0:CAP], ACT.Silu).then_inc(ex_sg, 1)
                act.wait_ge(ex_h, n + 1)
                if not first:
                    act.wait_ge(ex_d, n - M + 1)
                act.activation(ex_hhi[0:k, m, :], ex_hid[0:k, (q + m) % 2, :], ACT.Copy).then_inc(ex_hi, 1)

            def rows_out(e, k, q):
                act.wait_ge(ex_d, M * e + M)
                if k is not None:
                    act.wait_ge(eo_out[q], 16 * k)
                act.activation(eo[q][:], ps_d[:, 2 * q:2 * q + 2, :], ACT.Copy).then_inc(ex_eo, 1)

            def step(e, k, q, first=False, last=False, evict=True):
                hidden(e, q, 0, first)
                if not first:
                    rows_out(e - 1, k - 1 + q if evict else None, 1 - q)
                hidden(e, q, 1, first)
                if not last:
                    weights_gu(e + 1, k + q, 1 - q)
                    tokens(e + 1, 1 - q)
                hidden(e, q, 2, first)
                if not last:
                    weights_d(e + 1, 1 - q)

            act.wait_ge(rt_key, 1)
            act.activation(r_exp[:], r_key[:], ACT.Exp).then_inc(r_exp_done, 1)
            for m in range(MS):
                sh(B - 1, m)
            weights_gu(0, 0, 0)
            act.wait_ge(routed, 1)
            weights_d(0, 0)
            act.wait_ge(sh_sum, B)
            tokens(0, 0)
            step(0, 0, 0, first=True)
            step(1, 0, 1, evict=False)
            step(2, 1, 0, evict=False)
            with act.Fori(1, E // 2 - 1) as r:
                step(2 * r + 1, r, 1)
                step(2 * r + 2, r + 1, 0)
            step(E - 1, E // 2 - 1, 1, last=True)
            rows_out(E - 1, E // 2 - 1, 1)

        @block.vector
        def _(dve):
            links = [0]

            def link(ins, b):
                links[0] += 1
                ins.then_inc(chain, 1)
                dve.wait_ge(chain, LINKS * b + links[0])

            dve.wait_ge(router_hi, 1)
            dve.tensor_tensor(gate_lo[:], ps_gu[:, 0, 0:C * E].rearrange("p (c e) -> p c e", c=C),
                              gate_hi[:].bitcast(F32), ALU.subtract).then_inc(router_lo, 1)

            def moments(b):
                for j in range(J):
                    last = dve.bn_stats(bn[:, j, :], x2[:, b, j, :])
                link(last, b)
                dve.memset(after_wait[:], 0.0)
                for j in range(J):
                    last = dve.bn_aggr(mv[:, j, :], bn[:, j, :])
                last.then_inc(var_done, 1)

            def normalise(b, n, dst, done):
                dve.wait_ge(rstd_done, 2 * n + 2)
                for j in range(J):
                    last = dve.tensor_scalar(dst[:, j, :], x2[:, b, j, :], mv[:, j, 0:1], small["rstd"][:, j:j + 1],
                                             ALU.subtract, ALU.mult)
                last.then_inc(done, 1)

            def largest(b, u0, n, dst):
                for c in range(n):
                    dve.wait_ge(unit_full, filled(b, u0 + c))
                    dve.tensor_reduce(small[dst][:, c:c + 1], bank(u0 + c), AX.X, ALU.max,
                                      apply_absolute_value=True).then_inc(unit_free[(u0 + c) % 2], 1)

            def smoothing(b, i, width, u_w, u_x):
                w, v = small["recip_w"], slice(0, width)
                dve.wait_ge(unit_free[(u_w + width - 1) % 2], read(b, u_w + width - 1))
                link(dve.tensor_scalar(w[:, v], small["amax_w"][:, v], Q_EPS, None, ALU.max), b)
                link(dve.reciprocal(w[:, v], w[:, v]), b)
                dve.wait_ge(unit_free[(u_x + width - 1) % 2], read(b, u_x + width - 1))
                dve.scalar_tensor_tensor(out=small["ratio"][:, v], in0=small["amax_x"][:, v], scalar=Q_EPS,
                                         in1=w[:, v], op0=ALU.max, op1=ALU.mult).then_inc(ratio_done, 1)
                dve.wait_ge(root_done, 2 * b + i + 1)
                link(dve.tensor_scalar(small["smooth"][:, v], small["root"][:, v], Q_EPS, None, ALU.max), b)
                link(dve.reciprocal(small["rsmooth"][:, v], small["smooth"][:, v]), b)

            def diagonal(src, j, at):
                return dve.tensor_scalar(diag[:, at * P:(at + 1) * P], ident[:], small[src][:, j:j + 1], None, ALU.mult)

            def step_sizes(b, which, src, width, done):
                link(dve.tensor_reduce(small[which + "_max"][:], src[:, :, 0:width], AX.X, ALU.max,
                                       apply_absolute_value=True), b)
                link(dve.tensor_scalar(small[which + "_step"][:], small[which + "_max"][:], Q_EPS, 1.0 / QMAX,
                                       ALU.max, ALU.mult), b)
                dve.reciprocal(small[which + "_inv"][:], small[which + "_step"][:]).then_inc(done, 1)

            def dequantise(b, u0, dst):
                dve.wait_ge(unit_free[(u0 - 1) % 2], read(b, u0 - 1))
                for j in range(J):
                    dve.wait_ge(unit_full, filled(b, u0 + j))
                    dve.scalar_tensor_tensor(out=dst[:, j, :], in0=bank(u0 + j), scalar=small["x_step"][:, j:j + 1],
                                             in1=row_w[:], op0=ALU.mult, op1=ALU.mult).then_inc(unit_free[(u0 + j) % 2], 1)

            def sh(f, m):
                n = MS * f + m
                k = P if m < MFULL else SREST
                dve.wait_ge(sh_sg, n + 1)
                up = ps_gu[:, 1, :] if m < MFULL else sh_rest[:]
                dve.tensor_tensor(sh_hid[0:k, m % 2, :], sh_silu[0:k, m % 2, :], up, ALU.mult).then_inc(sh_h, 1)
                dve.wait_ge(sh_hi, n + 1)
                dve.tensor_tensor(sh_hlo[0:k, m % RING, :], sh_hid[0:k, m % 2, :],
                                  sh_hhi[0:k, m % RING, :].bitcast(F32), ALU.subtract).then_inc(sh_lo, 1)

            def sh_add(f):
                dve.wait_ge(sh_ring, RING + MS * f + MS)
                for j in range(J):
                    last = dve.scalar_tensor_tensor(out=x2[:, f, j, :], in0=ps_d[:, j, :], scalar=tg[:, 1:2],
                                                    in1=x2[:, f, j, :], op0=ALU.mult, op1=ALU.add)
                last.then_inc(sh_sum, 1)

            def sequence(b, f):
                links[0] = 0

                def sh_chunk(m):
                    if f is not None:
                        sh(f, m)

                dve.wait_ge(x_in, 16 if f is None else 32)
                largest(b, U_WT, C, "amax_w")
                moments(b)
                normalise(b, 2 * b, xn, xn_done)
                largest(b, U_XT, C, "amax_x")
                sh_chunk(0)
                smoothing(b, 0, C, U_WT, U_XT)
                for c in range(C):
                    last = diagonal("smooth", c, c)
                last.then_inc(smooth_diag, 1)
                dve.wait_ge(unit_full, filled(b, U_S))
                for c in range(C):
                    last = diagonal("rsmooth", c, c)
                last.then_inc(smooth_diag, 1)
                sh_chunk(1)
                if f is not None:
                    dve.wait_ge(x2n_out, 16 * b)
                dve.wait_ge(unit_full, filled(b, U_RS))
                dve.tensor_tensor(xs[:], xn[:], bank(U_RS).unsqueeze(1).broadcast_to((P, J, D)),
                                  ALU.mult).then_inc(unit_free[U_RS % 2], 1)
                dve.wait_ge(unit_free[U_RS % 2], read(b, U_RS))
                step_sizes(b, "x", xs, D, x_steps)
                dve.wait_ge(ws_done, 2 * b + 1)
                step_sizes(b, "w", ws, D, w_steps)
                dve.wait_ge(w_steps, 2 * b + 1)
                for j in range(J):
                    last = diagonal("w_step", j, j)
                last.then_inc(step_diag, 1)
                sh_chunk(2)
                dequantise(b, U_H, xn)
                sh_chunk(3)
                dve.wait_ge(silu_done, b + 1)
                dve.tensor_tensor(gated[:], gated[:], xn[:, :, I2:D], ALU.mult).then_inc(gated_done, 1)
                largest(b, U_W2T, C2, "amax_w")
                largest(b, U_AT, C2, "amax_x")
                smoothing(b, 1, C2, U_W2T, U_AT)
                for c in range(C2):
                    diagonal("smooth", c, c)
                    last = diagonal("rsmooth", c, C2 + c)
                last.then_inc(smooth_diag, 1)
                sh_chunk(4)
                dve.wait_ge(unit_free[U_S2 % 2], read(b, U_S2))
                link(dve.tensor_tensor(xs[:, :, 0:I2], gated[:], row_s[:, I2:D].unsqueeze(1).broadcast_to((P, J, I2)),
                                       ALU.mult), b)
                step_sizes(b, "x", xs, I2, x_steps)
                dve.wait_ge(ws_done, 2 * b + 2)
                step_sizes(b, "w", ws, I2, w_steps)
                dve.wait_ge(w_steps, 2 * b + 2)
                for j in range(J):
                    last = diagonal("w_step", j, j)
                last.then_inc(step_diag, 1)
                sh_chunk(5)
                dequantise(b, U_Y, xn)
                dve.wait_ge(unit_free[(U_Y + J - 1) % 2], read(b, U_Y + J - 1))
                link(dve.tensor_tensor(x2[:, b], x2[:, b], xn[:], ALU.add), b)
                dve.memset(after_wait[:], 0.0)
                moments(b)
                if f is not None:
                    sh_add(f)
                normalise(b, 2 * b + 1, xs, x2n_done)
                for c in range(C):
                    dve.wait_ge(xt_hi_done, C * b + c + 1)
                    dve.tensor_tensor(xt_lo[:, c, :], bank(U_X2T + c), xt_hi[:, c, :].bitcast(F32),
                                      ALU.subtract).then_inc(unit_free[(U_X2T + c) % 2], 1)
                assert links[0] == LINKS, links[0]

            sequence(0, None)
            with dve.Fori(1, B) as b:
                sequence(b, b - 1)

            steps = [0]

            def then(ins):
                steps[0] += 1
                ins.then_inc(rt, 1)
                dve.wait_ge(rt, steps[0])

            def per_tile(ap):
                return ap.unsqueeze(2).broadcast_to((P, NT, E))

            last_f = B - 1
            rev = rev_e[:].unsqueeze(1).broadcast_to((P, NT, E))
            T_MAX, T_SUM, T_E, T_W, T_POS = 0, 1, 2, 4, 6

            def top(k):
                return r_top[:, k, :]

            dve.wait_ge(unit_free[U_LG % 2], read(B - 1, U_LG))
            then(dve.tensor_reduce(top(T_MAX), lg[:], AX.X, ALU.max))
            then(dve.tensor_tensor(r_key[:], lg[:], per_tile(top(T_MAX)), ALU.subtract))
            then(dve.tensor_scalar(r_key[:], r_key[:], EXP_MIN, None, ALU.max))
            dve.tensor_copy(r_tmp[:], r_key[:]).then_inc(rt_key, 1)
            dve.wait_ge(rt_key, 1)
            for k in range(2):
                then(dve.tensor_reduce(top(T_MAX), r_tmp[:], AX.X, ALU.max))
                then(dve.tensor_tensor(r_cnt[:], r_tmp[:], per_tile(top(T_MAX)), ALU.is_equal))
                then(dve.tensor_tensor(r_cnt[:], r_cnt[:], rev, ALU.mult))
                then(dve.tensor_reduce(top(T_E + k), r_cnt[:], AX.X, ALU.max))
                then(dve.tensor_tensor(r_oh[k][:], rev, per_tile(top(T_E + k)), ALU.is_equal))
                if k == 0:
                    then(dve.scalar_tensor_tensor(out=r_tmp[:], in0=r_oh[0][:], scalar=4 * EXP_MIN, in1=r_tmp[:],
                                                  op0=ALU.mult, op1=ALU.add))
            then(dve.tensor_tensor(r_cnt[:], r_oh[0][:], r_oh[1][:], ALU.add))
            then(dve.tensor_reduce(r_seq[:, 0], r_cnt[:].rearrange("p (b j) e -> p b e j", j=J), AX.X, ALU.add))
            then(dve.memset(r_seq[:, 1, 0, :], 0.0))
            for b in range(1, B):
                last = dve.tensor_tensor(r_seq[:, 1, b, :], r_seq[:, 1, b - 1, :], r_seq[:, 0, b - 1, :], ALU.add)
                then(last) if b < B - 1 else last.then_inc(seq_done, 1)
            sh(last_f, 0)
            sh(last_f, 1)
            dve.wait_ge(rank_done, 1)
            cnt = r_cnt[:].rearrange("p (b j) e -> p b j e", j=J)
            rank = r_rank[:].rearrange("p (b j) e -> p b j e", j=J)
            then(dve.tensor_copy(rank[:, :, 0, :], ps_a[:, 0, 0:B * E].rearrange("p (b e) -> p b e", e=E)))
            for j in range(1, J):
                then(dve.tensor_tensor(rank[:, :, j, :], rank[:, :, j - 1, :], cnt[:, :, j - 1, :], ALU.add))
            for k in range(2):
                then(dve.tensor_tensor(r_tmp[:], r_oh[k][:], r_rank[:], ALU.mult))
                then(dve.tensor_reduce(top(T_POS + k), r_tmp[:], AX.X, ALU.add))
                then(dve.tensor_tensor(r_tok[k][:], r_oh[k][:], per_tile(tok_no[:]), ALU.mult))
            for n in range(2 * NT):
                i, k = divmod(n, 2)
                if n >= 4:
                    dve.wait_ge(table_mm, n - 3)
                dve.tensor_scalar(pos_oh[:, n % 4, :], slot_no[:], top(T_POS + k)[:, i:i + 1], None,
                                  ALU.is_equal).then_inc(pos_done, 1)
                if n == 9:
                    sh(last_f, 2)
                if n == 19:
                    sh(last_f, 3)
            dve.wait_ge(table_mm, 2 * NT)
            for h in range(HALF):
                last = dve.tensor_copy(idx[:, h, :], ps_a[:, h, 0:E])
            last.then_inc(idx_ready, 1)
            sh(last_f, 4)
            for k in range(2):
                then(dve.tensor_scalar(top(T_POS + k), top(T_POS + k), float(CAP - 1), float(E * CAP), ALU.min, ALU.add))
                then(dve.scalar_tensor_tensor(out=top(T_POS + k), in0=top(T_E + k), scalar=-float(CAP),
                                              in1=top(T_POS + k), op0=ALU.mult, op1=ALU.add))
                then(dve.tensor_copy(slots[:, k, :], top(T_POS + k)))
            dve.wait_ge(r_exp_done, 1)
            then(dve.tensor_reduce(top(T_SUM), r_exp[:], AX.X, ALU.add))
            then(dve.reciprocal(top(T_SUM), top(T_SUM)))
            for k in range(2):
                then(dve.tensor_tensor(r_tmp[:], r_exp[:], r_oh[k][:], ALU.mult))
                then(dve.tensor_reduce(top(T_W + k), r_tmp[:], AX.X, ALU.add))
                last = dve.scalar_tensor_tensor(out=wts[:, k, :], in0=top(T_W + k), scalar=tg[:, 1:2], in1=top(T_SUM),
                                                op0=ALU.mult, op1=ALU.mult)
            last.then_inc(routed, 1)
            sh(last_f, 5)
            sh_add(last_f)

            def weights_d(e, q):
                dve.wait_ge(ex_wdhi, e + 1)
                dve.tensor_tensor(wd_lo[q][:, 0:M - 1, :], raw_d[q][:, 0:M - 1, :], wd_hi[q][:, 0:M - 1, :].bitcast(F32),
                                  ALU.subtract)
                k = ROWS[M - 1]
                dve.tensor_tensor(wd_lo[q][0:k, M - 1, :], raw_d[q][0:k, M - 1, :], wd_hi[q][0:k, M - 1, :].bitcast(F32),
                                  ALU.subtract).then_inc(ex_wdlo, 1)

            def tokens(e, q):
                dve.wait_ge(ex_xh, e + 1)
                dve.tensor_tensor(ex_xlo[q][:], ps_xt, ex_xhi[q][:].bitcast(F32), ALU.subtract).then_inc(ex_x, 1)

            def hidden(e, q, m):
                n, k = M * e + m, ROWS[m]
                dve.wait_ge(ex_sg, n + 1)
                dve.tensor_tensor(ex_hid[0:k, (q + m) % 2, :], ex_silu[0:k, (q + m) % 2, :],
                                  ps_gu[0:k, (q + m) % 2, CAP:2 * CAP], ALU.mult).then_inc(ex_h, 1)
                dve.wait_ge(ex_hi, n + 1)
                dve.tensor_tensor(ex_hlo[0:k, m, :], ex_hid[0:k, (q + m) % 2, :], ex_hhi[0:k, m, :].bitcast(F32),
                                  ALU.subtract).then_inc(ex_lo, 1)

            def step(e, q, last=False):
                hidden(e, q, 0)
                hidden(e, q, 1)
                if not last:
                    tokens(e + 1, 1 - q)
                hidden(e, q, 2)
                if not last:
                    weights_d(e + 1, 1 - q)

            weights_d(0, 0)
            tokens(0, 0)
            step(0, 0)
            with dve.Fori(0, E // 2 - 1) as r:
                step(2 * r + 1, 1)
                step(2 * r + 2, 0)
            step(E - 1, 1, last=True)

            def add_rows(b, r, k):
                dve.wait_ge(got_in[k], 16 * 2 * J * (r + 1))
                x2_b, w_b = x2[:, b], wts[:].rearrange("p n (b j) -> p b n j", j=J)[:, b]
                for j in range(J):
                    last = dve.scalar_tensor_tensor(out=x2_b[:, j, :], in0=got[:, k, j, 0, :], scalar=w_b[:, 0, j:j + 1],
                                                    in1=x2_b[:, j, :], op0=ALU.mult, op1=ALU.add)
                last.then_inc(sum_half, 1)
                dve.wait_ge(sum_half, b + 1)
                for j in range(J):
                    last = dve.scalar_tensor_tensor(out=x2_b[:, j, :], in0=got[:, k, j, 1, :], scalar=w_b[:, 1, j:j + 1],
                                                    in1=x2_b[:, j, :], op0=ALU.mult, op1=ALU.add)
                last.then_inc(summed, 1)

            with dve.Fori(0, B // 2) as r:
                for k in range(2):
                    add_rows(2 * r + k, r, k)

        @block.tensor
        def _(pe):
            def three(dst, a_hi, a_lo, b_hi, b_lo, start, stop):
                pe.matmul(dst, a_hi, b_hi, start=start, stop=False)
                pe.matmul(dst, a_hi, b_lo, start=False, stop=False)
                return pe.matmul(dst, a_lo, b_hi, start=False, stop=stop)

            pe.wait_ge(masks_ready, 2)
            pe.wait_ge(router_in, 16)
            for c in range(C):
                last = pe.transpose(ps_gu[:, 0, c * E:(c + 1) * E], gate_row[:, c * P:(c + 1) * P], ident[0:E, 0:E])
            last.then_inc(router_t, 1)

            def free(b, u):
                if u >= 2 or not (isinstance(b, int) and b == 0):
                    pe.wait_ge(unit_free[u % 2], UNITS // 2 * b + u // 2)

            def turned(b, u0, n, src):
                for c in range(n):
                    free(b, u0 + c)
                    for j in range(J):
                        last = pe.transpose(bank(u0 + c)[:, j * P:(j + 1) * P], src[:, j, c * P:(c + 1) * P], ident[:])
                    last.then_inc(unit_full, 1)

            def row(b, u, sem_, count):
                pe.wait_ge(sem_, count)
                free(b, u)
                pe.matmul(bank(u), ones[:], diag[:], start=True, stop=True).then_inc(unit_full, 1)

            def integer_product(b, u0, n, qx, qw):
                for j in range(J):
                    free(b, u0 + j)
                    for c in range(n):
                        last = pe.matmul(bank(u0 + j), qx[:, c, j * P:(j + 1) * P], qw[:, c, :], start=(c == 0), stop=(c == n - 1))
                    last.then_inc(unit_full, 1)

            def sh_up(f, m):
                n = MS * f + m
                if m == 0:
                    pe.wait_ge(unit_free[(U_X2T + C - 1) % 2], read(f, U_X2T + C - 1))
                else:
                    pe.wait_ge(sh_h, n)
                parts = ((0, m * P), (1, (MFULL + m) * P)) if m < MFULL else ((0, 2 * MFULL * P),)
                for u, at in parts:
                    for c in range(C):
                        last = three(ps_gu[:, u, :], sw_hi[:, c, at:at + P], sw_lo[:, c, at:at + P],
                                     xt_hi[:, c, :], xt_lo[:, c, :], c == 0, c == C - 1)
                last.then_inc(sh_gu, 1)

            def sh_down(f, m):
                n = MS * f + m
                k = P if m < MFULL else SREST
                pe.wait_ge(sh_lo, n + 1)
                for j in range(J):
                    t = slice(j * P, (j + 1) * P)
                    last = three(ps_d[:, j, :], sh_hhi[0:k, m % RING, t], sh_hlo[0:k, m % RING, t],
                                 sd_hi[0:k, m, :], sd_lo[0:k, m, :], m == 0, m == MS - 1)
                last.then_inc(sh_ring, 1)

            def sequence(b, f):
                def up(m):
                    if f is not None:
                        sh_up(f, m)

                def down(m):
                    if f is not None:
                        sh_down(f, m)

                pe.wait_ge(w1_in, 16 * b + 16)
                turned(b, U_WT, C, w1)
                pe.wait_ge(xn_done, b + 1)
                turned(b, U_XT, C, xn)
                up(0)
                row(b, U_S, smooth_diag, 3 * b + 1)
                row(b, U_RS, smooth_diag, 3 * b + 2)
                up(1)
                down(0)
                pe.wait_ge(qx_done, 2 * b + 1)
                turned(b, U_QX, C, xs)
                pe.wait_ge(qw_done, 2 * b + 1)
                turned(b, U_QW, C, ws)
                row(b, U_WSTEP, step_diag, 2 * b + 1)
                up(2)
                down(1)
                for u in (U_QX + C - 1, U_QW + C - 1):
                    pe.wait_ge(unit_free[u % 2], read(b, u))
                integer_product(b, U_H, C, q_x, q_w)
                up(3)
                down(2)
                pe.wait_ge(w2_in, 16 * b + 16)
                turned(b, U_W2T, C2, w2)
                pe.wait_ge(gated_done, b + 1)
                turned(b, U_AT, C2, gated)
                up(4)
                down(3)
                row(b, U_S2, smooth_diag, 3 * b + 3)
                up(5)
                down(4)
                pe.wait_ge(qx_done, 2 * b + 2)
                turned(b, U_QA, C2, xs)
                pe.wait_ge(qw_done, 2 * b + 2)
                turned(b, U_QW2, C2, ws)
                row(b, U_W2STEP, step_diag, 2 * b + 2)
                down(5)
                for u in (U_QA + C2 - 1, U_QW2 + C2 - 1):
                    pe.wait_ge(unit_free[u % 2], read(b, u))
                integer_product(b, U_Y, C2, q_x2, q_w2)
                pe.wait_ge(x2n_done, b + 1)
                turned(b, U_X2T, C, xs)
                free(b, U_LG)
                u = U_X2T + C - 1
                pe.wait_ge(unit_free[u % 2], read(b, u))
                if f is None:
                    pe.wait_ge(router_lo, 1)
                for j in range(J):
                    t = slice(j * P, (j + 1) * P)
                    for c in range(C):
                        last = three(bank(U_LG)[:, j * E:(j + 1) * E], xt_hi[:, c, t], xt_lo[:, c, t],
                                     gate_hi[:, c, :], gate_lo[:, c, :], c == 0, c == C - 1)
                last.then_inc(unit_full, 1)

            pe.sem_inc(sh_ring, RING)
            sequence(0, None)
            pe.wait_ge(sgu_hi, 1)
            pe.wait_ge(sgu_lo, 2)
            pe.wait_ge(sdn_hi, 1)
            pe.wait_ge(sdn_lo, 1)
            with pe.Fori(1, B) as b:
                sequence(b, b - 1)

            f = B - 1
            sh_up(f, 0)
            sh_up(f, 1)
            sh_down(f, 0)
            pe.wait_ge(seq_done, 1)
            pe.matmul(ps_a[:, 0, 0:B * E], before[:], r_seq[:, 0].rearrange("p b e -> p (b e)"), start=True, stop=False)
            pe.matmul(ps_a[:, 0, 0:B * E], ones[:], r_seq[:, 1].rearrange("p b e -> p (b e)"), start=False,
                      stop=True).then_inc(rank_done, 1)
            sh_up(f, 2)
            sh_down(f, 1)

            def table(n0, n1):
                for n in range(n0, n1):
                    i, k = divmod(n, 2)
                    pe.wait_ge(pos_done, n + 1)
                    for h in range(HALF):
                        last = pe.matmul(ps_a[:, h, 0:E], pos_oh[:, n % 4, h * P:(h + 1) * P], r_tok[k][:, i, :],
                                         start=(n == 0), stop=(n == 2 * NT - 1))
                    last.then_inc(table_mm, 1)

            table(0, 10)
            sh_up(f, 3)
            sh_down(f, 2)
            table(10, 20)
            sh_up(f, 4)
            sh_down(f, 3)
            table(20, 2 * NT)
            sh_up(f, 5)
            sh_down(f, 4)
            sh_down(f, 5)

            def turn_tokens(e, k, q):
                pe.wait_ge(xg_in[q], 32 * k + 32)
                for c in range(C):
                    for h in range(HALF):
                        last = pe.transpose(ps_xt[:, c, h * P:(h + 1) * P], xg[q][:, h, c * P:(c + 1) * P], ident[:])
                last.then_inc(ex_xt, 1)

            def up(e, q, m, first=False):
                n, k = M * e + m, ROWS[m]
                if m == 0:
                    pe.wait_ge(ex_x, e + 1)
                    pe.wait_ge(ex_whi, e + 1)
                    pe.wait_ge(ex_wlo, e + 1)
                if not first or m == 2:
                    pe.wait_ge(ex_h, n - 1)
                u = (q + m) % 2
                for g in range(2):
                    for c in range(C):
                        i = slice(m * P, m * P + k)
                        last = three(ps_gu[0:k, u, g * CAP:(g + 1) * CAP], w_hi[q][:, g, c, i], w_lo[q][:, g, c, i],
                                     ex_xhi[q][:, c, :], ex_xlo[q][:, c, :], c == 0, c == C - 1)
                last.then_inc(ex_gu, 1)

            def down(e, q, m, evicted=True):
                n, k = M * e + m, ROWS[m]
                pe.wait_ge(ex_lo, n + 1)
                if m == 0:
                    pe.wait_ge(ex_wdlo, e + 1)
                    if evicted:
                        pe.wait_ge(ex_eo, e - 1)
                for h in range(HALF):
                    t = slice(h * P, (h + 1) * P)
                    last = three(ps_d[:, 2 * q + h, :], ex_hhi[0:k, m, t], ex_hlo[0:k, m, t],
                                 wd_hi[q][0:k, m, :], wd_lo[q][0:k, m, :], m == 0, m == M - 1)
                last.then_inc(ex_d, 1)

            def step(e, k, q, first=False, last=False, evicted=True):
                up(e, q, 0, first)
                if not first:
                    down(e - 1, 1 - q, 2)
                up(e, q, 1, first)
                down(e, q, 0, evicted)
                if not last:
                    turn_tokens(e + 1, k + q, 1 - q)
                up(e, q, 2, first)
                down(e, q, 1)

            pe.wait_ge(idx_ready, 1)
            turn_tokens(0, 0, 0)
            pe.wait_ge(sh_sum, B)
            step(0, 0, 0, first=True, evicted=False)
            step(1, 0, 1, evicted=False)
            step(2, 1, 0)
            with pe.Fori(1, E // 2 - 1) as r:
                step(2 * r + 1, r, 1)
                step(2 * r + 2, r + 1, 0)
            step(E - 1, E // 2 - 1, 1, last=True)
            down(E - 1, 1, 2)


_INS = ['x', 'fside_BxS2xS2_0', 'ctx_1024', 'g_xattn', 'g_ffn', 'L0_ffn_gate_w', 'L0_ffn_w_gate', 'L0_ffn_w_up',
        'L0_ffn_w_down', 'L0_ffn_ws_gate', 'L0_ffn_ws_up', 'L0_ffn_ws_down']


def kernel(**inputs):
    import numpy as _np
    import concourse.bacc as _bacc
    from concourse import mybir as _mybir
    from concourse.bass_utils import run_bass_kernel_spmd as _run

    nc = _bacc.Bacc("TRN2", target_bir_lowering=False, num_devices=1)
    arrays, args = {}, []
    for name in _INS:
        a = _np.ascontiguousarray(inputs[name])
        arrays[f"in_{name}"] = a
        args.append(nc.dram_tensor(f"in_{name}", a.shape, _mybir.dt.from_np(a.dtype), kind="ExternalInput").ap())
    out = nc.dram_tensor("out", inputs["x"].shape, _mybir.dt.float32, kind="ExternalOutput").ap()
    flamingo_block(nc, *args, out)
    r = _run(nc, [arrays], core_ids=[0])
    return r.results[0]["out"]
```

```python
from contextlib import ExitStack

import concourse.bass as bass
from concourse import mybir

ALU = mybir.AluOpType
ACT = mybir.ActivationFunctionType
AX = mybir.AxisListType
F32 = mybir.dt.float32
R32 = mybir.dt.float32r
BF16 = mybir.dt.bfloat16
U32 = mybir.dt.uint32

P = 128
BANK = 512
LN_EPS = 1e-5
Q_EPS = 1e-6
QMAX = 127.0
MAGIC = 12582912.0
EXP_MIN = -87.33654


def flamingo_block(nc, x, guw, dw, g_x, g_f, gate_w, w_gate, w_up, w_down, s_gate, s_up, s_down, out):
    B, T, D = x.shape
    I2 = dw.shape[2]
    E, _, I = w_gate.shape
    IS = s_gate.shape[1]
    CAP = 256
    HALF = CAP // P
    J = T // P
    C = D // P
    C2 = I2 // P
    NT = B * J
    M = -(-I // P)
    ROWS = [min(P, I - m * P) for m in range(M)]
    MFULL = IS // P
    SREST = IS - MFULL * P
    MS = MFULL + 1
    GU = 2 * IS
    assert T == BANK and D == BANK and 2 * SREST == P and 2 * I2 == D and HALF == 2 and M == 3 and E % 2 == 0

    x_v = x.rearrange("b (p j) d -> b p j d", j=J)
    out_v = out.rearrange("b (p j) d -> b p j d", j=J)
    guw_v = guw.rearrange("b (j p) d -> b p j d", p=P)
    dw_v = dw.rearrange("b (j p) d -> b p j d", p=P)
    wg_v = w_gate.rearrange("e (c p) i -> e p c i", p=P)
    wu_v = w_up.rearrange("e (c p) i -> e p c i", p=P)
    sg_v = s_gate.rearrange("(c p) i -> p c i", p=P)
    su_v = s_up.rearrange("(c p) i -> p c i", p=P)

    x2n_dram = nc.dram_tensor("x2n_scratch", (B * T, D), F32).ap()
    eo_dram = nc.dram_tensor("expert_out_scratch", (E * CAP, D), F32).ap()
    x2n_v = x2n_dram.rearrange("(b p j) d -> b p j d", p=P, j=J)
    eo_v = eo_dram.rearrange("(e h p) d -> e p h d", h=HALF, p=P)

    base = -(-nc.sbuf_base // 32) * 32

    def place(cursor, name, shape, dt=F32):
        n = 2 if dt == BF16 else 4
        for k in shape[1:]:
            n *= k
        at = cursor[0]
        cursor[0] += -(-n // 32) * 32
        return nc.alloc_sbuf_tensor_at(name, shape, dt, offset=at)

    cur = [base]
    x2 = place(cur, "x2", [P, B, J, D])
    ident = place(cur, "ident", [P, P])
    ident_b = place(cur, "ident_b", [P, P], BF16)
    ones = place(cur, "ones", [P, P])
    before = place(cur, "before", [P, P])
    slot_no = place(cur, "slot_no", [P, CAP])
    rev_e = place(cur, "rev_e", [P, E])
    tok_no = place(cur, "tok_no", [P, NT])
    powers = place(cur, "powers", [P, 2, J])
    ln_eps = place(cur, "ln_eps", [P, J])
    after_wait = place(cur, "after_wait", [P, 1])
    tg = place(cur, "tg", [P, 2])
    lg = place(cur, "lg", [P, NT, E])
    gate_hi = place(cur, "gate_hi", [P, C, E], R32)
    gate_lo = place(cur, "gate_lo", [P, C, E], R32)
    wts = place(cur, "wts", [P, 2, NT])
    slots = place(cur, "slots", [P, 2, NT], U32)
    slot_col = place(cur, "slot_col", [P, 2, J, 2], U32)
    idx = place(cur, "idx", [P, HALF, E], U32)
    idx_col = place(cur, "idx_col", [P, 2, HALF], U32)

    region = cur[0]
    w1 = place(cur, "w1", [P, J, D])
    xn = place(cur, "xn", [P, J, D])
    xr = place(cur, "xr", [P, J, D], BF16)
    wr = place(cur, "wr", [P, J, D], BF16)
    q_x = place(cur, "q_x", [P, C, T], BF16)
    q_w = place(cur, "q_w", [P, C, D], BF16)
    diag_a = place(cur, "diag_a", [P, D])
    row_s_a = place(cur, "row_s_a", [P, D])
    row_r_a = place(cur, "row_r_a", [P, D])
    row_w_a = place(cur, "row_w_a", [P, D])
    y = place(cur, "y", [P, J, D])
    route = cur[0]
    w2 = place(cur, "w2", [P, J, I2])
    gated = place(cur, "gated", [P, J, I2])
    ar = place(cur, "ar", [P, J, I2], BF16)
    wr2 = place(cur, "wr2", [P, J, I2], BF16)
    q_a = place(cur, "q_a", [P, C2, T], BF16)
    q_w2 = place(cur, "q_w2", [P, C2, D], BF16)
    diag_b = place(cur, "diag_b", [P, D])
    row_s_b = place(cur, "row_s_b", [P, I2])
    row_r_b = diag_b[:, I2:2 * I2]
    row_w_b = place(cur, "row_w_b", [P, D])
    bn = [place(cur, f"bn_{n}", [P, J, 6]) for n in "ab"]
    mv = [place(cur, f"mv_{n}", [P, J, 2]) for n in "ab"]
    small = [{n: place(cur, f"{n}_{layer}", [P, J]) for n in (
        "var_eps", "rstd", "amax_w", "amax_x", "recip_w", "ratio", "root", "smooth",
        "x_max", "w_max", "x_step", "x_inv", "w_step", "w_inv")} for layer in "ab"]
    shared = cur[0]
    xt_hi = place(cur, "xt_hi", [P, C, T], R32)
    xt_lo = place(cur, "xt_lo", [P, C, T], R32)
    sgu_at = cur[0]
    sw_lo = place(cur, "sw_lo", [P, C, GU], R32)
    sw_hi = place(cur, "sw_hi", [P, C, GU], R32)
    sd_at = cur[0]
    sd_lo = place(cur, "sd_lo", [P, MS, D], R32)
    sd_hi = place(cur, "sd_hi", [P, MS, D], R32)
    sh_hhi = place(cur, "sh_hhi", [P, 3, T], R32)
    sh_hlo = place(cur, "sh_hlo", [P, 3, T], R32)
    sh_hid = place(cur, "sh_hid", [P, 2, T])
    raw_sgu = place([sgu_at], "raw_sgu", [P, C, GU])
    raw_sd = place([sd_at], "raw_sd", [P, MS, D])

    cur = [route]
    r_key = place(cur, "r_key", [P, NT, E])
    r_exp = place(cur, "r_exp", [P, NT, E])
    r_oh = [place(cur, f"r_oh{k}", [P, NT, E]) for k in range(2)]
    r_tmp = place(cur, "r_tmp", [P, NT, E])
    r_cnt = place(cur, "r_cnt", [P, NT, E])
    r_rank = place(cur, "r_rank", [P, NT, E])
    r_tok = [place(cur, f"r_tok{k}", [P, NT, E]) for k in range(2)]
    r_seq = place(cur, "r_seq", [P, 2, B, E])
    r_top = place(cur, "r_top", [P, 12, NT])
    pos_oh = place(cur, "pos_oh", [P, 4, CAP])
    assert cur[0] <= shared

    cur = [region]
    raw_gu, raw_d, w_hi, w_lo, wd_hi, wd_lo, ex_xhi, ex_xlo, eo, xg = ([None, None] for _ in range(10))
    raw_gu[0] = place(cur, "raw_gu0", [P, 2, C, I])
    raw_d[0] = place(cur, "raw_d0", [P, M, D])
    w_hi[0] = place(cur, "w_hi0", [P, 2, C, I], R32)
    w_lo[0] = place(cur, "w_lo0", [P, 2, C, I], R32)
    xg[0] = place(cur, "xg0", [P, HALF, D])
    assert cur[0] <= route
    cur = [route]
    xg[1] = place(cur, "xg1", [P, HALF, D])
    wd_hi[0] = place(cur, "wd_hi0", [P, M, D], R32)
    wd_lo[0] = place(cur, "wd_lo0", [P, M, D], R32)
    assert cur[0] <= shared
    cur = [shared]
    raw_gu[1] = place(cur, "raw_gu1", [P, 2, C, I])
    raw_d[1] = place(cur, "raw_d1", [P, M, D])
    w_hi[1] = place(cur, "w_hi1", [P, 2, C, I], R32)
    w_lo[1] = place(cur, "w_lo1", [P, 2, C, I], R32)
    wd_hi[1] = place(cur, "wd_hi1", [P, M, D], R32)
    wd_lo[1] = place(cur, "wd_lo1", [P, M, D], R32)
    ex_xhi[0] = place(cur, "ex_xhi0", [P, C, CAP], R32)
    ex_xlo[0] = place(cur, "ex_xlo0", [P, C, CAP], R32)
    assert cur[0] <= sd_at
    cur = [sd_at]
    ex_xhi[1] = place(cur, "ex_xhi1", [P, C, CAP], R32)
    ex_xlo[1] = place(cur, "ex_xlo1", [P, C, CAP], R32)
    for q in range(2):
        eo[q] = place(cur, f"eo{q}", [P, HALF, D])
    ex_hhi = place(cur, "ex_hhi", [P, M, CAP], R32)
    ex_hlo = place(cur, "ex_hlo", [P, M, CAP], R32)
    ex_silu = place(cur, "ex_silu", [P, 2, CAP])
    ex_hid = place(cur, "ex_hid", [P, 2, CAP])
    cur = [region]
    got = place(cur, "got", [P, 2, J, 2, D])

    A_WT, A_XT, A_S, A_QX, A_QW, A_WSTEP, A_H, A_UNITS = 0, 1, 2, 3, 5, 7, 8, 12
    B_T, B_S, B_QA, B_QW, B_WSTEP, B_Y, B_X2T, B_LG, B_UNITS = 0, 1, 2, 3, 4, 5, 9, 13, 14
    LINKS_A, LINKS_B = 10, 11
    RING = 3

    with ExitStack() as ctx:
        def sem(name):
            return ctx.enter_context(nc.semaphore(name))

        ps_a = ctx.enter_context(nc.psum_tensor("ps_a", [P, 2, BANK], F32))
        ps_gu = ctx.enter_context(nc.psum_tensor("ps_gu", [P, 2, BANK], F32))
        ps_d = ctx.enter_context(nc.psum_tensor("ps_d", [P, 4, BANK], F32))
        ps_xt = ps_a[:, :, :].rearrange("p u (c n) -> p (u c) n", n=CAP)

        x_in, w1_in, w2_in, gates_in, router_in = (sem(n) for n in ("x_in", "w1_in", "w2_in", "gates_in", "router_in"))
        sgu_in, sd_in = sem("sgu_in"), sem("sd_in")
        x2n_out = sem("x2n_out")
        const_ready, masks_ready, tanh_done = sem("const_ready"), sem("masks_ready"), sem("tanh_done")
        router_t, router_hi, router_lo = sem("router_t"), sem("router_hi"), sem("router_lo")
        sgu_hi, sgu_lo, sdn_hi, sdn_lo = sem("sgu_hi"), sem("sgu_lo"), sem("sdn_hi"), sem("sdn_lo")
        full, free = [sem("full_a"), sem("full_b")], [sem("free_a"), sem("free_b")]
        chain, var_done, rstd_done, ratio_done, root_done, pm_done = (
            [sem(f"{n}_{layer}") for layer in "ab"]
            for n in ("chain", "var_done", "rstd_done", "ratio_done", "root_done", "pm_done"))
        smooth_diag, step_diag, ws_done, x_steps, w_steps, x_scaled, w_scaled, qx_done, qw_done = (
            [sem(f"{n}_{layer}") for layer in "ab"]
            for n in ("smooth_diag", "step_diag", "ws_done", "x_steps", "w_steps", "x_scaled", "w_scaled",
                      "qx_done", "qw_done"))
        xn_done, pmx_done, silu_done, gated_done = sem("xn_done"), sem("pmx_done"), sem("silu_done"), sem("gated_done")
        x2n_done, xt_hi_done = sem("x2n_done"), sem("xt_hi_done")
        sh_gu, sh_sg, sh_h, sh_hi, sh_lo, sh_ring, sh_sum = (
            sem(n) for n in ("sh_gu", "sh_sg", "sh_h", "sh_hi", "sh_lo", "sh_ring", "sh_sum"))
        rt_key = sem("rt_key")
        rt, r_exp_done, seq_done, rank_done = sem("rt"), sem("r_exp_done"), sem("seq_done"), sem("rank_done")
        pos_done, table_mm, idx_ready, routed = (
            sem("pos_done"), sem("table_mm"), sem("idx_ready"), sem("routed"))
        raw_in = [sem("raw_in0"), sem("raw_in1")]
        xg_in = [sem("xg_in0"), sem("xg_in1")]
        eo_out = [sem("eo_out0"), sem("eo_out1")]
        col_done, ex_xt, ex_xh, ex_x = sem("col_done"), sem("ex_xt"), sem("ex_xh"), sem("ex_x")
        ex_whi, ex_wlo, ex_wdhi, ex_wdlo = sem("ex_whi"), sem("ex_wlo"), sem("ex_wdhi"), sem("ex_wdlo")
        ex_gu, ex_sg, ex_h, ex_hi, ex_lo, ex_d, ex_eo = (
            sem(n) for n in ("ex_gu", "ex_sg", "ex_h", "ex_hi", "ex_lo", "ex_d", "ex_eo"))
        cols_staged = sem("cols_staged")
        slot_cols, got_in, sum_half, summed, out_done = (
            sem("slot_cols"), [sem("got_in0"), sem("got_in1")], sem("sum_half"), sem("summed"), sem("out_done"))

        block = ctx.enter_context(nc.Block())

        LA, LB = 0, 1
        COUNT = (A_UNITS, B_UNITS)

        def bank(layer):
            return ps_a[:, layer, :]

        def unit(layer, b, u):
            return COUNT[layer] * b + u + 1

        @block.sync
        def _(sp):
            def load_w1(b):
                sp.dma_start(w1[:], guw_v[b]).then_inc(w1_in, 16)

            def load_w2(b):
                sp.dma_start(w2[:], dw_v[b]).then_inc(w2_in, 16)

            def load_raw(e, q):
                sp.dma_start(raw_gu[q][:, 0], wg_v[e]).then_inc(raw_in[q], 16)
                sp.dma_start(raw_gu[q][:, 1], wu_v[e]).then_inc(raw_in[q], 16)
                sp.dma_start(raw_d[q][:, 0:M - 1, :],
                             w_down[e, 0:(M - 1) * P, :].rearrange("(m p) d -> p m d", p=P)).then_inc(raw_in[q], 16)
                sp.dma_start(raw_d[q][0:ROWS[M - 1], M - 1, :], w_down[e, (M - 1) * P:I, :]).then_inc(raw_in[q], 16)

            def store_x2n(b):
                sp.wait_ge(x2n_done, b + 1)
                sp.dma_start(x2n_v[b], y[:]).then_inc(x2n_out, 16)

            def store_eo(e, q):
                sp.wait_ge(ex_eo, e + 1)
                sp.dma_start(eo_v[e], eo[q][:]).then_inc(eo_out[q], 16)

            sp.dma_start(x2[:, 0], x_v[0]).then_inc(x_in, 16)
            load_w1(0)
            sp.dma_start(y[0:E, 0, :], gate_w).then_inc(router_in, 16)
            sp.dma_start(tg[:, 0:1], g_x.rearrange("(a n) -> a n", a=1).broadcast_to((P, 1))).then_inc(gates_in, 16)
            sp.dma_start(tg[:, 1:2], g_f.rearrange("(a n) -> a n", a=1).broadcast_to((P, 1))).then_inc(gates_in, 16)
            load_w2(0)
            sp.dma_start(x2[:, 1:B], x_v[1:B].rearrange("b p j d -> p b j d")).then_inc(x_in, 16)
            whole, rest = slice(0, MFULL * P), slice(MFULL * P, IS)
            for n, (src, part, at) in enumerate(((sg_v, whole, 0), (su_v, whole, MFULL * P),
                                                 (sg_v, rest, 2 * MFULL * P), (su_v, rest, 2 * MFULL * P + SREST))):
                width = part.stop - part.start
                sp.dma_start(raw_sgu[:, :, at:at + width], src[:, :, part]).then_inc(sgu_in, 16)
            sp.dma_start(raw_sd[:, 0:MFULL, :],
                         s_down[0:MFULL * P, :].rearrange("(m p) d -> p m d", p=P)).then_inc(sd_in, 16)
            sp.dma_start(raw_sd[0:SREST, MFULL, :], s_down[MFULL * P:IS, :]).then_inc(sd_in, 16)
            sp.wait_ge(qw_done[LA], 1)
            load_w1(1)
            with sp.Fori(1, B - 1) as r:
                sp.wait_ge(qw_done[LB], r)
                load_w2(r)
                sp.wait_ge(qw_done[LA], r + 1)
                load_w1(r + 1)
                store_x2n(r - 1)
            sp.wait_ge(qw_done[LB], B - 1)
            load_w2(B - 1)
            store_x2n(B - 2)
            sp.wait_ge(gated_done, B)
            load_raw(0, 0)
            store_x2n(B - 1)
            sp.wait_ge(sh_gu, MS * B)
            load_raw(1, 1)

            def step(e, q):
                sp.wait_ge(ex_whi, e + 1)
                sp.wait_ge(ex_wlo, e + 1)
                sp.wait_ge(ex_wdhi, e + 1)
                sp.wait_ge(ex_wdlo, e + 1)
                load_raw(e + 2, q)

            step(0, 0)
            with sp.Fori(0, E // 2 - 2) as r:
                step(2 * r + 1, 1)
                store_eo(2 * r, 0)
                step(2 * r + 2, 0)
                store_eo(2 * r + 1, 1)
            step(E - 3, 1)
            for e in range(E - 4, E):
                store_eo(e, e % 2)
            sp.wait_ge(eo_out[0], 16 * (E // 2))
            sp.wait_ge(eo_out[1], 16 * (E // 2))
            with sp.Fori(0, B) as b:
                sp.wait_ge(summed, b + 1)
                sp.dma_start(out_v[b], x2[:, b]).then_inc(out_done, 16)
            sp.wait_ge(out_done, 16 * B)

        @block.gpsimd
        def _(pool):
            pool.memset(ident[:], 0.0).then_inc(const_ready, 1)
            pool.memset(ones[:], 1.0).then_inc(const_ready, 1)
            pool.memset(powers[:, 0, :], 0.5).then_inc(const_ready, 1)
            pool.memset(powers[:, 1, :], -0.5).then_inc(const_ready, 1)
            pool.memset(ln_eps[:], LN_EPS).then_inc(const_ready, 1)
            pool.iota(slot_no[:], [[1, CAP]], base=0, channel_multiplier=0,
                      allow_small_or_imprecise_dtypes=True).then_inc(const_ready, 1)
            pool.iota(rev_e[:], [[-1, E]], base=E, channel_multiplier=0,
                      allow_small_or_imprecise_dtypes=True).then_inc(const_ready, 1)
            pool.iota(tok_no[:], [[T, B], [1, J]], base=0, channel_multiplier=J,
                      allow_small_or_imprecise_dtypes=True).then_inc(const_ready, 1)
            pool.wait_ge(const_ready, 8)
            pool.affine_select(out=ident[:], in_=ident[:], compare_op=ALU.not_equal, fill=1.0, base=0,
                               pattern=[[-1, P]], channel_multiplier=1).then_inc(masks_ready, 1)
            pool.affine_select(out=before[:], in_=ones[:], compare_op=ALU.is_gt, fill=0.0, base=0,
                               pattern=[[1, P]], channel_multiplier=-1).then_inc(masks_ready, 1)
            pool.wait_ge(masks_ready, 2)
            pool.tensor_copy(ident_b[:], ident[:]).then_inc(masks_ready, 1)

            def norm_scale(layer, b):
                sm, done = small[layer], rstd_done[layer]
                pool.wait_ge(var_done[layer], b + 1)
                pool.tensor_tensor(sm["var_eps"][:], mv[layer][:, :, 1], ln_eps[:], ALU.add).then_inc(done, 1)
                pool.wait_ge(done, 2 * b + 1)
                pool.tensor_tensor(sm["rstd"][:], sm["var_eps"][:], powers[:, 1, :], ALU.pow).then_inc(done, 1)

            def root(layer, b, width):
                sm = small[layer]
                pool.wait_ge(ratio_done[layer], b + 1)
                pool.tensor_tensor(sm["root"][:, 0:width], sm["ratio"][:, 0:width], powers[:, 0, 0:width],
                                   ALU.pow).then_inc(root_done[layer], 1)

            def smooth_weights(layer, b, w, row, width, u):
                pool.wait_ge(free[layer], unit(layer, b, u))
                pool.tensor_tensor(w[:], w[:], row[:].unsqueeze(1).broadcast_to((P, J, width)),
                                   ALU.mult).then_inc(ws_done[layer], 1)

            def split_shared(c0, c1):
                pool.wait_ge(sgu_hi, 1)
                pool.tensor_tensor(sw_lo[:, c0:c1, :], raw_sgu[:, c0:c1, :], sw_hi[:, c0:c1, :].bitcast(F32),
                                   ALU.subtract).then_inc(sgu_lo, 1)

            def split_shared_down():
                pool.wait_ge(sdn_hi, 1)
                pool.tensor_tensor(sd_lo[:, 0:MFULL, :], raw_sd[:, 0:MFULL, :], sd_hi[:, 0:MFULL, :].bitcast(F32),
                                   ALU.subtract)
                pool.tensor_tensor(sd_lo[0:SREST, MFULL, :], raw_sd[0:SREST, MFULL, :],
                                   sd_hi[0:SREST, MFULL, :].bitcast(F32), ALU.subtract).then_inc(sdn_lo, 1)

            def iteration(a, b, split_here=False):
                if a is not None:
                    norm_scale(LA, a)
                if b is not None:
                    root(LB, b, C2)
                    smooth_weights(LB, b, w2, row_s_b, I2, B_S)
                if a is not None:
                    root(LA, a, C)
                    smooth_weights(LA, a, w1, row_s_a, D, A_S)
                if split_here:
                    split_shared(C // 2, C)
                if b is not None:
                    norm_scale(LB, b)

            iteration(0, None)
            split_shared(0, C // 2)
            iteration(1, 0, split_here=True)
            split_shared_down()
            with pool.Fori(2, B) as r:
                iteration(r, r - 1)
            iteration(None, B - 1)

            def gather(e, q):
                pool.tensor_copy(idx_col[:, q, :], idx[:, :, e]).then_inc(col_done, 1)
                pool.wait_ge(col_done, e + 1)
                pool.sem_inc(cols_staged, 1)
                for h in range(HALF):
                    pool.indirect_dma_start(xg[q][:, h, :], None, x2n_dram,
                                            bass.IndirectOffsetOnAxis(idx_col[:, q, h:h + 1], 0)).then_inc(xg_in[q], 16)

            def split(e, q):
                pool.wait_ge(ex_whi, e + 1)
                pool.tensor_tensor(w_lo[q][:], raw_gu[q][:], w_hi[q][:].bitcast(F32), ALU.subtract).then_inc(ex_wlo, 1)

            pool.wait_ge(x2n_out, 16 * B)
            pool.wait_ge(free[LB], unit(LB, B - 1, B_LG))
            split(0, 0)
            pool.wait_ge(idx_ready, 1)
            pool.wait_ge(routed, 1)
            gather(0, 0)
            gather(1, 1)

            def step(e, q):
                split(e + 1, 1 - q)
                pool.wait_ge(ex_xt, e + 1)
                gather(e + 2, q)

            step(0, 0)
            with pool.Fori(0, E // 2 - 2) as r:
                step(2 * r + 1, 1)
                step(2 * r + 2, 0)
            step(E - 3, 1)
            split(E - 1, 1)

            pool.wait_ge(eo_out[0], 16 * (E // 2))
            pool.wait_ge(eo_out[1], 16 * (E // 2))

            def gather_rows(b, k):
                pool.tensor_copy(slot_col[:, k].rearrange("p j n -> p n j"),
                                 slots[:].rearrange("p n (b j) -> p b n j", j=J)[:, b]).then_inc(slot_cols, 1)
                pool.wait_ge(slot_cols, b + 1)
                pool.sem_inc(cols_staged, 1)
                for j in range(J):
                    for n in range(2):
                        pool.indirect_dma_start(got[:, k, j, n, :], None, eo_dram,
                                                bass.IndirectOffsetOnAxis(slot_col[:, k, j, n:n + 1], 0)).then_inc(got_in[k], 16)

            gather_rows(0, 0)
            gather_rows(1, 1)
            with pool.Fori(1, B // 2) as r:
                for k in range(2):
                    pool.wait_ge(summed, 2 * r + k - 1)
                    gather_rows(2 * r + k, k)

        @block.scalar
        def _(act):
            act.wait_ge(gates_in, 32)
            act.activation(tg[:], tg[:], ACT.Tanh).then_inc(tanh_done, 1)
            act.wait_ge(router_t, 1)
            act.activation(gate_hi[:], ps_gu[:, 0, 0:C * E].rearrange("p (c e) -> p c e", c=C),
                           ACT.Copy).then_inc(router_hi, 1)

            def split_shared():
                act.wait_ge(sgu_in, 64)
                act.activation(sw_hi[:], raw_sgu[:], ACT.Copy).then_inc(sgu_hi, 1)

            def split_shared_down():
                act.wait_ge(sd_in, 32)
                act.activation(sd_hi[:, 0:MFULL, :], raw_sd[:, 0:MFULL, :], ACT.Copy)
                act.activation(sd_hi[0:SREST, MFULL, :], raw_sd[0:SREST, MFULL, :], ACT.Copy).then_inc(sdn_hi, 1)

            def copy_row(layer, b, u, dst, width, scale=1.0):
                act.wait_ge(full[layer], unit(layer, b, u))
                act.activation(dst[:], bank(layer)[:, 0:width], ACT.Copy, scale=scale).then_inc(free[layer], 1)

            def quantise(b, src, inv, dst, steps, scaled, done):
                act.wait_ge(steps, b + 1)
                for j in range(J):
                    last = act.activation(src[:, j, :], src[:, j, :], ACT.Copy, bias=MAGIC, scale=inv[:, j:j + 1])
                last.then_inc(scaled, 1)
                act.wait_ge(scaled, b + 1)
                act.activation(dst[:], src[:], ACT.Copy, bias=-MAGIC).then_inc(done, 1)

            def integers(layer, b, u0, n, dst):
                for u in range(n // 2):
                    act.wait_ge(full[layer], unit(layer, b, u0 + u))
                    act.activation(dst[:, 2 * u:2 * u + 2, :], bank(layer).bitcast(BF16).rearrange("p (c t) -> p c t", c=2),
                                   ACT.Copy).then_inc(free[layer], 1)

            def layer_silu(a):
                act.wait_ge(free[LA], unit(LA, a, A_H + J - 1))
                act.activation(gated[:], xn[:, :, 0:I2], ACT.Silu).then_inc(silu_done, 1)

            def x_hi(b):
                for c in range(C):
                    act.wait_ge(full[LB], unit(LB, b, B_X2T + c))
                    act.activation(xt_hi[:, c, :], bank(LB), ACT.Copy).then_inc(xt_hi_done, 1)

            def logits(b):
                act.wait_ge(full[LB], unit(LB, b, B_LG))
                act.activation(lg[:].rearrange("p (b j) e -> p b (j e)", j=J)[:, b], bank(LB)[:, 0:J * E],
                               ACT.Copy).then_inc(free[LB], 1)

            def sh(f, m):
                n = MS * f + m
                k = P if m < MFULL else SREST
                act.wait_ge(sh_gu, n + 1)
                if m == MFULL:
                    act.wait_ge(sh_lo, n)
                    act.activation(sh_hid[0:SREST, 1 - m % 2, :], ps_gu[SREST:P, 0, :], ACT.Copy)
                act.activation(sh_hid[0:k, m % 2, :], ps_gu[0:k, 0, :], ACT.Silu).then_inc(sh_sg, 1)
                act.wait_ge(sh_h, n + 1)
                act.wait_ge(sh_ring, n + 1)
                act.activation(sh_hhi[0:k, m % RING, :], sh_hid[0:k, m % 2, :], ACT.Copy).then_inc(sh_hi, 1)

            def iteration(a, b, f):
                def sh_chunk(m):
                    if f is not None:
                        sh(f, m)

                sh_chunk(0)
                sh_chunk(1)
                if b is not None:
                    copy_row(LB, b, B_S, row_s_b, I2)
                    quantise(b, gated, small[LB]["x_inv"], ar, x_steps[LB], x_scaled[LB], qx_done[LB])
                sh_chunk(2)
                if a is not None:
                    copy_row(LA, a, A_S, row_s_a, D)
                if b is not None:
                    quantise(b, w2, small[LB]["w_inv"], wr2, w_steps[LB], w_scaled[LB], qw_done[LB])
                    integers(LB, b, B_QA, C2, q_a)
                    integers(LB, b, B_QW, C2, q_w2)
                if a is not None:
                    quantise(a, xn, small[LA]["x_inv"], xr, x_steps[LA], x_scaled[LA], qx_done[LA])
                sh_chunk(3)
                if a is not None:
                    integers(LA, a, A_QX, C, q_x)
                if b is not None:
                    copy_row(LB, b, B_WSTEP, row_w_b, D, scale=tg[:, 0:1])
                if a is not None:
                    quantise(a, w1, small[LA]["w_inv"], wr, w_steps[LA], w_scaled[LA], qw_done[LA])
                sh_chunk(4)
                if a is not None:
                    integers(LA, a, A_QW, C, q_w)
                    copy_row(LA, a, A_WSTEP, row_w_a, D)
                sh_chunk(5)
                if b is not None:
                    x_hi(b)
                if a is not None:
                    layer_silu(a)
                if b is not None:
                    logits(b)

            act.wait_ge(tanh_done, 1)
            iteration(0, None, None)
            split_shared()
            iteration(1, 0, None)
            split_shared_down()
            with act.Fori(2, B) as r:
                iteration(r, r - 1, r - 2)
            iteration(None, B - 1, B - 2)

            def weights_gu(e, k, q):
                act.wait_ge(raw_in[q], 64 * k + 64)
                act.activation(w_hi[q][:], raw_gu[q][:], ACT.Copy).then_inc(ex_whi, 1)

            def weights_d(e, q):
                act.activation(wd_hi[q][:, 0:M - 1, :], raw_d[q][:, 0:M - 1, :], ACT.Copy)
                act.activation(wd_hi[q][0:ROWS[M - 1], M - 1, :], raw_d[q][0:ROWS[M - 1], M - 1, :],
                               ACT.Copy).then_inc(ex_wdhi, 1)

            def tokens(e, q):
                act.wait_ge(ex_xt, e + 1)
                act.activation(ex_xhi[q][:], ps_xt, ACT.Copy).then_inc(ex_xh, 1)

            def hidden(e, q, m, first):
                n, k = M * e + m, ROWS[m]
                act.wait_ge(ex_gu, n + 1)
                act.activation(ex_silu[0:k, (q + m) % 2, :], ps_gu[0:k, (q + m) % 2, 0:CAP], ACT.Silu).then_inc(ex_sg, 1)
                act.wait_ge(ex_h, n + 1)
                if not first:
                    act.wait_ge(ex_d, n - M + 1)
                act.activation(ex_hhi[0:k, m, :], ex_hid[0:k, (q + m) % 2, :], ACT.Copy).then_inc(ex_hi, 1)

            def rows_out(e, k, q):
                act.wait_ge(ex_d, M * e + M)
                if k is not None:
                    act.wait_ge(eo_out[q], 16 * k)
                act.activation(eo[q][:], ps_d[:, 2 * q:2 * q + 2, :], ACT.Copy).then_inc(ex_eo, 1)

            def step(e, k, q, first=False, last=False, evict=True):
                if not last:
                    weights_gu(e + 1, k + q, 1 - q)
                hidden(e, q, 0, first)
                if not first:
                    rows_out(e - 1, k - 1 + q if evict else None, 1 - q)
                hidden(e, q, 1, first)
                if not last:
                    tokens(e + 1, 1 - q)
                hidden(e, q, 2, first)
                if not last:
                    weights_d(e + 1, 1 - q)

            act.wait_ge(rt_key, 1)
            act.activation(r_exp[:], r_key[:], ACT.Exp).then_inc(r_exp_done, 1)
            for m in range(MS):
                sh(B - 1, m)
                if m == 1:
                    weights_gu(0, 0, 0)
            act.wait_ge(routed, 1)
            weights_d(0, 0)
            tokens(0, 0)
            act.wait_ge(sh_sum, B)
            step(0, 0, 0, first=True)
            step(1, 0, 1, evict=False)
            step(2, 1, 0, evict=False)
            with act.Fori(1, E // 2 - 1) as r:
                step(2 * r + 1, r, 1)
                step(2 * r + 2, r + 1, 0)
            step(E - 1, E // 2 - 1, 1, last=True)
            rows_out(E - 1, E // 2 - 1, 1)

        @block.vector
        def _(dve):
            links = [0, 0]
            LINKS = (LINKS_A, LINKS_B)

            def link(ins, layer, b):
                links[layer] += 1
                ins.then_inc(chain[layer], 1)
                dve.wait_ge(chain[layer], LINKS[layer] * b + links[layer])

            dve.wait_ge(router_hi, 1)
            dve.tensor_tensor(gate_lo[:], ps_gu[:, 0, 0:C * E].rearrange("p (c e) -> p c e", c=C),
                              gate_hi[:].bitcast(F32), ALU.subtract).then_inc(router_lo, 1)

            def partial(src, dst):
                return dve.tensor_reduce(dst, src.rearrange("p j d -> p d j"), AX.X, ALU.max, apply_absolute_value=True)

            def moments(layer, b, n):
                for j in range(J):
                    last = dve.bn_stats(bn[layer][:, j, :], x2[:, n, j, :])
                link(last, layer, b)
                dve.memset(after_wait[:], 0.0)
                for j in range(J):
                    last = dve.bn_aggr(mv[layer][:, j, :], bn[layer][:, j, :])
                last.then_inc(var_done[layer], 1)

            def normalise(layer, b, dst, done):
                dve.wait_ge(rstd_done[layer], 2 * b + 2)
                for j in range(J):
                    last = dve.tensor_scalar(dst[:, j, :], x2[:, b, j, :], mv[layer][:, j, 0:1],
                                             small[layer]["rstd"][:, j:j + 1], ALU.subtract, ALU.mult)
                last.then_inc(done, 1)

            def largest(layer, b, u, dst, width):
                dve.wait_ge(full[layer], unit(layer, b, u))
                dve.tensor_reduce(dst, bank(layer)[:, 0:width * P].rearrange("p (c q) -> p c q", q=P), AX.X,
                                  ALU.max).then_inc(free[layer], 1)

            def ratio(layer, b, u, w_max, x_max):
                sm, width = small[layer], w_max.shape[1]
                w = sm["recip_w"][:, 0:width]
                dve.wait_ge(free[layer], unit(layer, b, u))
                link(dve.tensor_scalar(w, w_max, Q_EPS, None, ALU.max), layer, b)
                link(dve.reciprocal(w, w), layer, b)
                dve.scalar_tensor_tensor(out=sm["ratio"][:, 0:width], in0=x_max, scalar=Q_EPS, in1=w,
                                         op0=ALU.max, op1=ALU.mult).then_inc(ratio_done[layer], 1)

            def diagonals(layer, diag, src, n):
                for c in range(n):
                    last = dve.tensor_scalar(diag[:, c * P:(c + 1) * P], ident[:], small[layer][src][:, c:c + 1], None,
                                             ALU.mult)
                return last

            def smoothing(layer, b, diag, n):
                sm = small[layer]
                dve.wait_ge(root_done[layer], b + 1)
                link(dve.tensor_scalar(sm["smooth"][:, 0:n], sm["root"][:, 0:n], Q_EPS, None, ALU.max), layer, b)
                diagonals(layer, diag, "smooth", n).then_inc(smooth_diag[layer], 1)

            def step_sizes(layer, b, which, src, done):
                sm = small[layer]
                link(dve.tensor_reduce(sm[which + "_max"][:], src[:], AX.X, ALU.max, apply_absolute_value=True), layer, b)
                link(dve.tensor_scalar(sm[which + "_step"][:], sm[which + "_max"][:], Q_EPS, 1.0 / QMAX,
                                       ALU.max, ALU.mult), layer, b)
                dve.reciprocal(sm[which + "_inv"][:], sm[which + "_step"][:]).then_inc(done, 1)

            def activation_steps(layer, b, src, row_s, row_r, width, u):
                dve.wait_ge(free[layer], unit(layer, b, u))
                link(dve.reciprocal(row_r[:], row_s[:]), layer, b)
                link(dve.tensor_tensor(src[:], src[:], row_r[:].unsqueeze(1).broadcast_to((P, J, width)), ALU.mult), layer, b)
                step_sizes(layer, b, "x", src, x_steps[layer])

            def weight_steps(layer, b, w, diag):
                dve.wait_ge(ws_done[layer], b + 1)
                step_sizes(layer, b, "w", w, w_steps[layer])
                diagonals(layer, diag, "w_step", J).then_inc(step_diag[layer], 1)

            def dequantise(layer, b, u0, j, row, dst):
                dve.wait_ge(full[layer], unit(layer, b, u0 + j))
                dve.scalar_tensor_tensor(out=dst[:, j, :], in0=bank(layer), scalar=small[layer]["x_step"][:, j:j + 1],
                                         in1=row[:], op0=ALU.mult, op1=ALU.mult).then_inc(free[layer], 1)

            def sh(f, m):
                n = MS * f + m
                k = P if m < MFULL else SREST
                dve.wait_ge(sh_sg, n + 1)
                up = ps_gu[:, 1, :] if m < MFULL else sh_hid[0:SREST, 1 - m % 2, :]
                dve.tensor_tensor(sh_hid[0:k, m % 2, :], sh_hid[0:k, m % 2, :], up, ALU.mult).then_inc(sh_h, 1)
                dve.wait_ge(sh_hi, n + 1)
                dve.tensor_tensor(sh_hlo[0:k, m % RING, :], sh_hid[0:k, m % 2, :],
                                  sh_hhi[0:k, m % RING, :].bitcast(F32), ALU.subtract).then_inc(sh_lo, 1)

            def sh_add(f):
                dve.wait_ge(sh_ring, RING + MS * f + MS)
                for j in range(J):
                    last = dve.scalar_tensor_tensor(out=x2[:, f, j, :], in0=ps_d[:, j, :], scalar=tg[:, 1:2],
                                                    in1=x2[:, f, j, :], op0=ALU.mult, op1=ALU.add)
                last.then_inc(sh_sum, 1)

            def iteration(a, b, f):
                links[:] = [0, 0]

                def sh_chunk(m):
                    if f is not None:
                        sh(f, m)

                if b is not None:
                    dve.wait_ge(w2_in, 16 * b + 16)
                    partial(w2[:], row_w_b[:, 0:I2])
                    dve.wait_ge(gated_done, b + 1)
                    partial(gated[:], row_w_b[:, I2:2 * I2]).then_inc(pm_done[LB], 1)
                if a is not None:
                    dve.wait_ge(x_in, 16 if b is None else 32)
                    dve.memset(after_wait[:], 0.0)
                    moments(LA, a, a)
                    dve.wait_ge(w1_in, 16 * a + 16)
                    partial(w1[:], row_w_a[:]).then_inc(pm_done[LA], 1)
                sh_chunk(0)
                if b is not None:
                    w_x = small[LB]["amax_w"]
                    largest(LB, b, B_T, w_x[:], 2 * C2)
                    ratio(LB, b, B_T, w_x[:, 0:C2], w_x[:, C2:2 * C2])
                if a is not None:
                    normalise(LA, a, xn, xn_done)
                if b is not None:
                    smoothing(LB, b, diag_b, C2)
                if a is not None:
                    dve.wait_ge(xn_done, a + 1)
                    partial(xn[:], diag_a[:]).then_inc(pmx_done, 1)
                    largest(LA, a, A_WT, small[LA]["amax_w"][:], C)
                sh_chunk(1)
                if b is not None:
                    activation_steps(LB, b, gated, row_s_b, row_r_b, I2, B_S)
                if a is not None:
                    largest(LA, a, A_XT, small[LA]["amax_x"][:], C)
                    ratio(LA, a, A_XT, small[LA]["amax_w"][:], small[LA]["amax_x"][:])
                if b is not None:
                    weight_steps(LB, b, w2, diag_b)
                if a is not None:
                    smoothing(LA, a, diag_a, C)
                sh_chunk(2)
                if a is not None:
                    activation_steps(LA, a, xn, row_s_a, row_r_a, D, A_S)
                sh_chunk(3)
                if a is not None:
                    weight_steps(LA, a, w1, diag_a)
                if b is not None:
                    if not (isinstance(b, int) and b == 0):
                        dve.wait_ge(x2n_out, 16 * b)
                    dve.wait_ge(free[LB], unit(LB, b, B_WSTEP))
                    for j in range(J):
                        dequantise(LB, b, B_Y, j, row_w_b, y)
                sh_chunk(4)
                if b is not None:
                    dve.wait_ge(free[LB], unit(LB, b, B_Y + J - 1))
                    link(dve.tensor_tensor(x2[:, b], x2[:, b], y[:], ALU.add), LB, b)
                    dve.memset(after_wait[:], 0.0)
                    moments(LB, b, b)
                sh_chunk(5)
                if b is not None:
                    normalise(LB, b, y, x2n_done)
                for c in range(C):
                    if b is not None:
                        dve.wait_ge(xt_hi_done, C * b + c + 1)
                        dve.tensor_tensor(xt_lo[:, c, :], bank(LB), xt_hi[:, c, :].bitcast(F32),
                                          ALU.subtract).then_inc(free[LB], 1)
                    if a is not None:
                        if c == 0:
                            dve.wait_ge(free[LA], unit(LA, a, A_WSTEP))
                        dequantise(LA, a, A_H, c, row_w_a, xn)
                if a is not None:
                    dve.wait_ge(silu_done, a + 1)
                    dve.tensor_tensor(gated[:], gated[:], xn[:, :, I2:D], ALU.mult).then_inc(gated_done, 1)
                if f is not None:
                    sh_add(f)
                assert links[LA] in (0, LINKS_A) and links[LB] in (0, LINKS_B), links

            iteration(0, None, None)
            iteration(1, 0, None)
            with dve.Fori(2, B) as r:
                iteration(r, r - 1, r - 2)
            iteration(None, B - 1, B - 2)

            steps = [0]

            def then(ins):
                steps[0] += 1
                ins.then_inc(rt, 1)
                dve.wait_ge(rt, steps[0])

            def per_tile(ap):
                return ap.unsqueeze(2).broadcast_to((P, NT, E))

            last_f = B - 1
            rev = rev_e[:].unsqueeze(1).broadcast_to((P, NT, E))
            T_MAX, T_SUM, T_E, T_W, T_POS = 0, 1, 2, 4, 6

            def top(k):
                return r_top[:, k, :]

            dve.wait_ge(free[LB], unit(LB, B - 1, B_LG))
            then(dve.tensor_reduce(top(T_MAX), lg[:], AX.X, ALU.max))
            then(dve.tensor_tensor(r_key[:], lg[:], per_tile(top(T_MAX)), ALU.subtract))
            then(dve.tensor_scalar(r_key[:], r_key[:], EXP_MIN, None, ALU.max))
            dve.tensor_copy(r_tmp[:], r_key[:]).then_inc(rt_key, 1)
            dve.wait_ge(rt_key, 1)
            for k in range(2):
                then(dve.tensor_reduce(top(T_MAX), r_tmp[:], AX.X, ALU.max))
                then(dve.tensor_tensor(r_cnt[:], r_tmp[:], per_tile(top(T_MAX)), ALU.is_equal))
                then(dve.tensor_tensor(r_cnt[:], r_cnt[:], rev, ALU.mult))
                then(dve.tensor_reduce(top(T_E + k), r_cnt[:], AX.X, ALU.max))
                then(dve.tensor_tensor(r_oh[k][:], rev, per_tile(top(T_E + k)), ALU.is_equal))
                if k == 0:
                    then(dve.scalar_tensor_tensor(out=r_tmp[:], in0=r_oh[0][:], scalar=4 * EXP_MIN, in1=r_tmp[:],
                                                  op0=ALU.mult, op1=ALU.add))
            then(dve.tensor_tensor(r_cnt[:], r_oh[0][:], r_oh[1][:], ALU.add))
            then(dve.tensor_reduce(r_seq[:, 0], r_cnt[:].rearrange("p (b j) e -> p b e j", j=J), AX.X, ALU.add))
            then(dve.memset(r_seq[:, 1, 0, :], 0.0))
            for b in range(1, B):
                last = dve.tensor_tensor(r_seq[:, 1, b, :], r_seq[:, 1, b - 1, :], r_seq[:, 0, b - 1, :], ALU.add)
                then(last) if b < B - 1 else last.then_inc(seq_done, 1)
            sh(last_f, 0)
            sh(last_f, 1)
            dve.wait_ge(rank_done, 1)
            cnt = r_cnt[:].rearrange("p (b j) e -> p b j e", j=J)
            rank = r_rank[:].rearrange("p (b j) e -> p b j e", j=J)
            then(dve.tensor_copy(rank[:, :, 0, :], ps_a[:, 0, 0:B * E].rearrange("p (b e) -> p b e", e=E)))
            for j in range(1, J):
                then(dve.tensor_tensor(rank[:, :, j, :], rank[:, :, j - 1, :], cnt[:, :, j - 1, :], ALU.add))
            for k in range(2):
                then(dve.tensor_tensor(r_tmp[:], r_oh[k][:], r_rank[:], ALU.mult))
                then(dve.tensor_reduce(top(T_POS + k), r_tmp[:], AX.X, ALU.add))
                then(dve.tensor_tensor(r_tok[k][:], r_oh[k][:], per_tile(tok_no[:]), ALU.mult))
            for n in range(2 * NT):
                i, k = divmod(n, 2)
                if n >= 4:
                    dve.wait_ge(table_mm, n - 3)
                dve.tensor_scalar(pos_oh[:, n % 4, :], slot_no[:], top(T_POS + k)[:, i:i + 1], None,
                                  ALU.is_equal).then_inc(pos_done, 1)
                if n == 9:
                    sh(last_f, 2)
                if n == 19:
                    sh(last_f, 3)
            dve.wait_ge(table_mm, 2 * NT)
            for h in range(HALF):
                last = dve.tensor_copy(idx[:, h, :], ps_a[:, h, 0:E])
            last.then_inc(idx_ready, 1)
            sh(last_f, 4)
            for k in range(2):
                then(dve.tensor_scalar(top(T_POS + k), top(T_POS + k), float(CAP - 1), float(E * CAP), ALU.min, ALU.add))
                then(dve.scalar_tensor_tensor(out=top(T_POS + k), in0=top(T_E + k), scalar=-float(CAP),
                                              in1=top(T_POS + k), op0=ALU.mult, op1=ALU.add))
                then(dve.tensor_copy(slots[:, k, :], top(T_POS + k)))
            dve.wait_ge(r_exp_done, 1)
            then(dve.tensor_reduce(top(T_SUM), r_exp[:], AX.X, ALU.add))
            then(dve.reciprocal(top(T_SUM), top(T_SUM)))
            for k in range(2):
                then(dve.tensor_tensor(r_tmp[:], r_exp[:], r_oh[k][:], ALU.mult))
                then(dve.tensor_reduce(top(T_W + k), r_tmp[:], AX.X, ALU.add))
                last = dve.scalar_tensor_tensor(out=wts[:, k, :], in0=top(T_W + k), scalar=tg[:, 1:2], in1=top(T_SUM),
                                                op0=ALU.mult, op1=ALU.mult)
            last.then_inc(routed, 1)
            sh(last_f, 5)
            sh_add(last_f)

            def weights_d(e, q):
                dve.wait_ge(ex_wdhi, e + 1)
                dve.tensor_tensor(wd_lo[q][:, 0:M - 1, :], raw_d[q][:, 0:M - 1, :], wd_hi[q][:, 0:M - 1, :].bitcast(F32),
                                  ALU.subtract)
                k = ROWS[M - 1]
                dve.tensor_tensor(wd_lo[q][0:k, M - 1, :], raw_d[q][0:k, M - 1, :], wd_hi[q][0:k, M - 1, :].bitcast(F32),
                                  ALU.subtract).then_inc(ex_wdlo, 1)

            def tokens(e, q):
                dve.wait_ge(ex_xh, e + 1)
                dve.tensor_tensor(ex_xlo[q][:], ps_xt, ex_xhi[q][:].bitcast(F32), ALU.subtract).then_inc(ex_x, 1)

            def hidden(e, q, m):
                n, k = M * e + m, ROWS[m]
                dve.wait_ge(ex_sg, n + 1)
                dve.tensor_tensor(ex_hid[0:k, (q + m) % 2, :], ex_silu[0:k, (q + m) % 2, :],
                                  ps_gu[0:k, (q + m) % 2, CAP:2 * CAP], ALU.mult).then_inc(ex_h, 1)
                dve.wait_ge(ex_hi, n + 1)
                dve.tensor_tensor(ex_hlo[0:k, m, :], ex_hid[0:k, (q + m) % 2, :], ex_hhi[0:k, m, :].bitcast(F32),
                                  ALU.subtract).then_inc(ex_lo, 1)

            def step(e, q, last=False):
                hidden(e, q, 0)
                hidden(e, q, 1)
                if not last:
                    tokens(e + 1, 1 - q)
                hidden(e, q, 2)
                if not last:
                    weights_d(e + 1, 1 - q)

            weights_d(0, 0)
            tokens(0, 0)
            step(0, 0)
            with dve.Fori(0, E // 2 - 1) as r:
                step(2 * r + 1, 1)
                step(2 * r + 2, 0)
            step(E - 1, 1, last=True)

            def add_rows(b, r, k):
                dve.wait_ge(got_in[k], 16 * 2 * J * (r + 1))
                x2_b, w_b = x2[:, b], wts[:].rearrange("p n (b j) -> p b n j", j=J)[:, b]
                for j in range(J):
                    last = dve.scalar_tensor_tensor(out=x2_b[:, j, :], in0=got[:, k, j, 0, :], scalar=w_b[:, 0, j:j + 1],
                                                    in1=x2_b[:, j, :], op0=ALU.mult, op1=ALU.add)
                last.then_inc(sum_half, 1)
                dve.wait_ge(sum_half, b + 1)
                for j in range(J):
                    last = dve.scalar_tensor_tensor(out=x2_b[:, j, :], in0=got[:, k, j, 1, :], scalar=w_b[:, 1, j:j + 1],
                                                    in1=x2_b[:, j, :], op0=ALU.mult, op1=ALU.add)
                last.then_inc(summed, 1)

            with dve.Fori(0, B // 2) as r:
                for k in range(2):
                    add_rows(2 * r + k, r, k)

        @block.tensor
        def _(pe):
            def three(dst, a_hi, a_lo, b_hi, b_lo, start, stop):
                pe.matmul(dst, a_hi, b_hi, start=start, stop=False)
                pe.matmul(dst, a_hi, b_lo, start=False, stop=False)
                return pe.matmul(dst, a_lo, b_hi, start=False, stop=stop)

            pe.wait_ge(masks_ready, 3)
            pe.wait_ge(router_in, 16)
            for c in range(C):
                last = pe.transpose(ps_gu[:, 0, c * E:(c + 1) * E], y[0:E, 0, c * P:(c + 1) * P], ident[0:E, 0:E])
            last.then_inc(router_t, 1)

            def empty(layer, b, u):
                if u > 0 or not (isinstance(b, int) and b == 0):
                    pe.wait_ge(free[layer], unit(layer, b, u) - 1)

            def turned_maxima(layer, b, u, sem_, src):
                pe.wait_ge(sem_, b + 1)
                empty(layer, b, u)
                for c in range(C):
                    last = pe.transpose(bank(layer)[:, c * P:(c + 1) * P], src[:, c * P:(c + 1) * P], ident[:])
                last.then_inc(full[layer], 1)

            def turned_integers(layer, b, u0, n, sem_, src):
                pe.wait_ge(sem_, b + 1)
                out16 = bank(layer).bitcast(BF16)
                for c in range(n):
                    if c % 2 == 0:
                        empty(layer, b, u0 + c // 2)
                    for j in range(J):
                        at = (c % 2 * J + j) * P
                        last = pe.transpose(out16[:, at:at + P], src[:, j, c * P:(c + 1) * P], ident_b[:])
                    if c % 2:
                        last.then_inc(full[layer], 1)

            def row(layer, b, u, sem_, diag, width):
                pe.wait_ge(sem_, b + 1)
                empty(layer, b, u)
                pe.matmul(bank(layer)[:, 0:width], ones[:], diag[:, 0:width], start=True, stop=True).then_inc(full[layer], 1)

            def integer_product(layer, b, u0, j, n, qx, qw):
                empty(layer, b, u0 + j)
                for c in range(n):
                    last = pe.matmul(bank(layer), qx[:, c, j * P:(j + 1) * P], qw[:, c, :], start=(c == 0), stop=(c == n - 1))
                last.then_inc(full[layer], 1)

            def sh_up(f, m, halves=(0, 1)):
                n = MS * f + m
                if halves[0] == 0:
                    if m == 0:
                        pe.wait_ge(free[LB], unit(LB, f, B_X2T + C - 1))
                    else:
                        pe.wait_ge(sh_h, n)
                parts = ((0, m * P), (1, (MFULL + m) * P)) if m < MFULL else ((0, 2 * MFULL * P),)
                for u, at in parts:
                    if u in halves:
                        for c in range(C):
                            last = three(ps_gu[:, u, :], sw_hi[:, c, at:at + P], sw_lo[:, c, at:at + P],
                                         xt_hi[:, c, :], xt_lo[:, c, :], c == 0, c == C - 1)
                if halves[-1] == 1:
                    last.then_inc(sh_gu, 1)

            def sh_down(f, m, tiles=(0, 1, 2, 3)):
                n = MS * f + m
                k = P if m < MFULL else SREST
                if tiles[0] == 0:
                    pe.wait_ge(sh_lo, n + 1)
                for j in tiles:
                    t = slice(j * P, (j + 1) * P)
                    last = three(ps_d[:, j, :], sh_hhi[0:k, m % RING, t], sh_hlo[0:k, m % RING, t],
                                 sd_hi[0:k, m, :], sd_lo[0:k, m, :], m == 0, m == MS - 1)
                if tiles[-1] == J - 1:
                    last.then_inc(sh_ring, 1)

            def iteration(a, b, f):
                def up(*chunk):
                    if f is not None:
                        sh_up(f, *chunk)

                def down(*chunk):
                    if f is not None:
                        sh_down(f, *chunk)

                def first_product(j):
                    if a is not None:
                        integer_product(LA, a, A_H, j, C, q_x, q_w)

                def second_product(j):
                    if b is not None:
                        integer_product(LB, b, B_Y, j, C2, q_a, q_w2)

                def turned_tokens(c):
                    if b is not None:
                        empty(LB, b, B_X2T + c)
                        for j in range(J):
                            last = pe.transpose(bank(LB)[:, j * P:(j + 1) * P], y[:, j, c * P:(c + 1) * P], ident[:])
                        last.then_inc(full[LB], 1)

                up(0)
                if b is not None:
                    turned_maxima(LB, b, B_T, pm_done[LB], row_w_b)
                if a is not None:
                    turned_maxima(LA, a, A_WT, pm_done[LA], row_w_a)
                up(1)
                if a is not None:
                    turned_maxima(LA, a, A_XT, pmx_done, diag_a)
                down(0)
                if b is not None:
                    row(LB, b, B_S, smooth_diag[LB], diag_b, I2)
                up(2)
                if a is not None:
                    row(LA, a, A_S, smooth_diag[LA], diag_a, D)
                down(1)
                if b is not None:
                    turned_integers(LB, b, B_QA, C2, qx_done[LB], ar)
                    turned_integers(LB, b, B_QW, C2, qw_done[LB], wr2)
                up(3)
                if a is not None:
                    turned_integers(LA, a, A_QX, C, qx_done[LA], xr)
                if b is not None:
                    row(LB, b, B_WSTEP, step_diag[LB], diag_b, D)
                second_product(0)
                up(4, (0,))
                second_product(1)
                up(4, (1,))
                second_product(2)
                down(2, (0, 1))
                second_product(3)
                down(2, (2, 3))
                if a is not None:
                    turned_integers(LA, a, A_QW, C, qw_done[LA], wr)
                    row(LA, a, A_WSTEP, step_diag[LA], diag_a, D)
                up(5)
                if b is not None:
                    pe.wait_ge(x2n_done, b + 1)
                turned_tokens(0)
                first_product(0)
                down(3, (0, 1))
                turned_tokens(1)
                first_product(1)
                down(3, (2, 3))
                turned_tokens(2)
                first_product(2)
                down(4, (0, 1))
                turned_tokens(3)
                first_product(3)
                down(4, (2, 3))
                down(5)
                if b is not None:
                    empty(LB, b, B_LG)
                    if isinstance(b, int) and b == 0:
                        pe.wait_ge(router_lo, 1)
                    for j in range(J):
                        t = slice(j * P, (j + 1) * P)
                        for c in range(C):
                            last = three(bank(LB)[:, j * E:(j + 1) * E], xt_hi[:, c, t], xt_lo[:, c, t],
                                         gate_hi[:, c, :], gate_lo[:, c, :], c == 0, c == C - 1)
                    last.then_inc(full[LB], 1)

            pe.sem_inc(sh_ring, RING)
            iteration(0, None, None)
            iteration(1, 0, None)
            pe.wait_ge(sgu_hi, 1)
            pe.wait_ge(sgu_lo, 2)
            pe.wait_ge(sdn_hi, 1)
            pe.wait_ge(sdn_lo, 1)
            with pe.Fori(2, B) as r:
                iteration(r, r - 1, r - 2)
            iteration(None, B - 1, B - 2)

            f = B - 1
            sh_up(f, 0)
            sh_up(f, 1)
            sh_down(f, 0)
            pe.wait_ge(seq_done, 1)
            pe.matmul(ps_a[:, 0, 0:B * E], before[:], r_seq[:, 0].rearrange("p b e -> p (b e)"), start=True, stop=False)
            pe.matmul(ps_a[:, 0, 0:B * E], ones[:], r_seq[:, 1].rearrange("p b e -> p (b e)"), start=False,
                      stop=True).then_inc(rank_done, 1)
            sh_up(f, 2)
            sh_down(f, 1)

            def table(n0, n1):
                for n in range(n0, n1):
                    i, k = divmod(n, 2)
                    pe.wait_ge(pos_done, n + 1)
                    for h in range(HALF):
                        last = pe.matmul(ps_a[:, h, 0:E], pos_oh[:, n % 4, h * P:(h + 1) * P], r_tok[k][:, i, :],
                                         start=(n == 0), stop=(n == 2 * NT - 1))
                    last.then_inc(table_mm, 1)

            table(0, 10)
            sh_up(f, 3)
            sh_down(f, 2)
            table(10, 20)
            sh_up(f, 4)
            sh_down(f, 3)
            table(20, 2 * NT)
            sh_up(f, 5)
            sh_down(f, 4)
            sh_down(f, 5)

            def turn_tokens(e, k, q):
                pe.wait_ge(xg_in[q], 32 * k + 32)
                for c in range(C):
                    for h in range(HALF):
                        last = pe.transpose(ps_xt[:, c, h * P:(h + 1) * P], xg[q][:, h, c * P:(c + 1) * P], ident[:])
                last.then_inc(ex_xt, 1)

            def up(e, q, m, first=False):
                n, k = M * e + m, ROWS[m]
                if m == 0:
                    pe.wait_ge(ex_x, e + 1)
                    pe.wait_ge(ex_whi, e + 1)
                    pe.wait_ge(ex_wlo, e + 1)
                if not first or m == 2:
                    pe.wait_ge(ex_h, n - 1)
                u = (q + m) % 2
                for g in range(2):
                    for c in range(C):
                        i = slice(m * P, m * P + k)
                        last = three(ps_gu[0:k, u, g * CAP:(g + 1) * CAP], w_hi[q][:, g, c, i], w_lo[q][:, g, c, i],
                                     ex_xhi[q][:, c, :], ex_xlo[q][:, c, :], c == 0, c == C - 1)
                last.then_inc(ex_gu, 1)

            def down(e, q, m, evicted=True):
                n, k = M * e + m, ROWS[m]
                pe.wait_ge(ex_lo, n + 1)
                if m == 0:
                    pe.wait_ge(ex_wdlo, e + 1)
                    if evicted:
                        pe.wait_ge(ex_eo, e - 1)
                for h in range(HALF):
                    t = slice(h * P, (h + 1) * P)
                    last = three(ps_d[:, 2 * q + h, :], ex_hhi[0:k, m, t], ex_hlo[0:k, m, t],
                                 wd_hi[q][0:k, m, :], wd_lo[q][0:k, m, :], m == 0, m == M - 1)
                last.then_inc(ex_d, 1)

            def step(e, k, q, first=False, last=False, evicted=True):
                up(e, q, 0, first)
                if not first:
                    down(e - 1, 1 - q, 2)
                up(e, q, 1, first)
                down(e, q, 0, evicted)
                if not last:
                    turn_tokens(e + 1, k + q, 1 - q)
                up(e, q, 2, first)
                down(e, q, 1)

            pe.wait_ge(idx_ready, 1)
            turn_tokens(0, 0, 0)
            pe.wait_ge(sh_sum, B)
            step(0, 0, 0, first=True, evicted=False)
            step(1, 0, 1, evicted=False)
            step(2, 1, 0)
            with pe.Fori(1, E // 2 - 1) as r:
                step(2 * r + 1, r, 1)
                step(2 * r + 2, r + 1, 0)
            step(E - 1, E // 2 - 1, 1, last=True)
            down(E - 1, 1, 2)


_INS = ['x', 'fside_BxS2xS2_0', 'ctx_1024', 'g_xattn', 'g_ffn', 'L0_ffn_gate_w', 'L0_ffn_w_gate', 'L0_ffn_w_up',
        'L0_ffn_w_down', 'L0_ffn_ws_gate', 'L0_ffn_ws_up', 'L0_ffn_ws_down']


def kernel(**inputs):
    import numpy as _np
    import concourse.bacc as _bacc
    from concourse import mybir as _mybir
    from concourse.bass_utils import run_bass_kernel_spmd as _run

    nc = _bacc.Bacc("TRN2", target_bir_lowering=False, num_devices=1)
    arrays, args = {}, []
    for name in _INS:
        a = _np.ascontiguousarray(inputs[name])
        arrays[f"in_{name}"] = a
        args.append(nc.dram_tensor(f"in_{name}", a.shape, _mybir.dt.from_np(a.dtype), kind="ExternalInput").ap())
    out = nc.dram_tensor("out", inputs["x"].shape, _mybir.dt.float32, kind="ExternalOutput").ap()
    flamingo_block(nc, *args, out)
    r = _run(nc, [arrays], core_ids=[0])
    return r.results[0]["out"]
```

```python
from contextlib import ExitStack

import concourse.bass as bass
from concourse import mybir

ALU = mybir.AluOpType
ACT = mybir.ActivationFunctionType
AX = mybir.AxisListType
F32 = mybir.dt.float32
R32 = mybir.dt.float32r
BF16 = mybir.dt.bfloat16
U32 = mybir.dt.uint32

P = 128
BANK = 512
LN_EPS = 1e-5
Q_EPS = 1e-6
QMAX = 127.0
MAGIC = 12582912.0
EXP_MIN = -87.33654


def flamingo_block(nc, x, guw, dw, g_x, g_f, gate_w, w_gate, w_up, w_down, s_gate, s_up, s_down, out):
    B, T, D = x.shape
    I2 = dw.shape[2]
    E, _, I = w_gate.shape
    IS = s_gate.shape[1]
    CAP = 256
    HALF = CAP // P
    J = T // P
    C = D // P
    C2 = I2 // P
    NT = B * J
    NPOS = 16
    M = -(-I // P)
    ROWS = [min(P, I - m * P) for m in range(M)]
    MFULL = IS // P
    SREST = IS - MFULL * P
    MS = MFULL + 1
    GU = 2 * IS
    assert T == BANK and D == BANK and 2 * SREST == P and 2 * I2 == D and HALF == 2 and M == 3 and E % 2 == 0

    x_v = x.rearrange("b (p j) d -> b p j d", j=J)
    out_v = out.rearrange("b (p j) d -> b p j d", j=J)
    guw_v = guw.rearrange("b (j p) d -> b p j d", p=P)
    dw_v = dw.rearrange("b (j p) d -> b p j d", p=P)
    wg_v = w_gate.rearrange("e (c p) i -> e p c i", p=P)
    wu_v = w_up.rearrange("e (c p) i -> e p c i", p=P)
    sg_v = s_gate.rearrange("(c p) i -> p c i", p=P)
    su_v = s_up.rearrange("(c p) i -> p c i", p=P)

    x2n_dram = nc.dram_tensor("x2n_scratch", (B * T, D), F32).ap()
    eo_dram = nc.dram_tensor("expert_out_scratch", (E * CAP, D), F32).ap()
    x2n_v = x2n_dram.rearrange("(b p j) d -> b p j d", p=P, j=J)
    eo_v = eo_dram.rearrange("(e h p) d -> e p h d", h=HALF, p=P)

    base = -(-nc.sbuf_base // 32) * 32

    def place(cursor, name, shape, dt=F32):
        n = 2 if dt == BF16 else 4
        for k in shape[1:]:
            n *= k
        at = cursor[0]
        cursor[0] += -(-n // 32) * 32
        return nc.alloc_sbuf_tensor_at(name, shape, dt, offset=at)

    cur = [base]
    x2 = place(cur, "x2", [P, B, J, D])
    ident = place(cur, "ident", [P, P])
    ident_b = place(cur, "ident_b", [P, P], BF16)
    ones = place(cur, "ones", [P, P])
    before = place(cur, "before", [P, P])
    slot_no = place(cur, "slot_no", [P, CAP])
    rev_e = place(cur, "rev_e", [P, E])
    tok_parts = place(cur, "tok_parts", [P, 3, NT])
    powers = place(cur, "powers", [P, 2, J])
    ln_eps = place(cur, "ln_eps", [P, J])
    after_wait = place(cur, "after_wait", [P, 1])
    tg = place(cur, "tg", [P, 2])
    lg = place(cur, "lg", [P, NT, E])
    gate_hi = place(cur, "gate_hi", [P, C, E], R32)
    gate_lo = place(cur, "gate_lo", [P, C, E], R32)
    wts = place(cur, "wts", [P, 2, NT])
    slots = place(cur, "slots", [P, 2, NT], U32)
    slot_col = place(cur, "slot_col", [P, 2, J, 2], U32)
    idx = place(cur, "idx", [P, HALF, E], U32)
    idx_col = place(cur, "idx_col", [P, 2, HALF], U32)

    region = cur[0]
    w1 = place(cur, "w1", [P, J, D])
    xn = place(cur, "xn", [P, J, D])
    xr = place(cur, "xr", [P, J, D], BF16)
    wr = place(cur, "wr", [P, J, D], BF16)
    q_x = place(cur, "q_x", [P, C, T], BF16)
    q_w = place(cur, "q_w", [P, C, D], BF16)
    diag_a = place(cur, "diag_a", [P, D])
    row_s_a = place(cur, "row_s_a", [P, D])
    row_w_a = place(cur, "row_w_a", [P, D])
    y = place(cur, "y", [P, J, D])
    route = cur[0]
    w2 = place(cur, "w2", [P, J, I2])
    gated = place(cur, "gated", [P, J, I2])
    ar = place(cur, "ar", [P, J, I2], BF16)
    wr2 = place(cur, "wr2", [P, J, I2], BF16)
    q_a = place(cur, "q_a", [P, C2, T], BF16)
    q_w2 = place(cur, "q_w2", [P, C2, D], BF16)
    diag_b = place(cur, "diag_b", [P, D])
    row_s_b = place(cur, "row_s_b", [P, D])
    row_w_b = place(cur, "row_w_b", [P, D])
    bn = [place(cur, f"bn_{n}", [P, J, 6]) for n in "ab"]
    mv = [place(cur, f"mv_{n}", [P, J, 2]) for n in "ab"]
    small = [{n: place(cur, f"{n}_{layer}", [P, J]) for n in (
        "var_eps", "rstd", "amax_w", "amax_x", "recip_w", "ratio", "root", "smooth", "rsmooth",
        "x_max", "w_max", "x_step", "x_inv", "w_step", "w_inv")} for layer in "ab"]
    shared = cur[0]
    xt_hi = place(cur, "xt_hi", [P, C, T], R32)
    xt_lo = place(cur, "xt_lo", [P, C, T], R32)
    sgu_at = cur[0]
    sw_lo = place(cur, "sw_lo", [P, C, GU], R32)
    sw_hi = place(cur, "sw_hi", [P, C, GU], R32)
    sd_at = cur[0]
    sd_lo = place(cur, "sd_lo", [P, MS, D], R32)
    sd_hi = place(cur, "sd_hi", [P, MS, D], R32)
    sh_hhi = place(cur, "sh_hhi", [P, 3, T], R32)
    sh_hlo = place(cur, "sh_hlo", [P, 3, T], R32)
    sh_hid = place(cur, "sh_hid", [P, 2, T])
    raw_sgu = place([sgu_at], "raw_sgu", [P, C, GU])
    raw_sd = place([sd_at], "raw_sd", [P, MS, D])

    cur = [route]
    r_key = place(cur, "r_key", [P, NT, E])
    r_exp = place(cur, "r_exp", [P, NT, E])
    r_oh = [place(cur, f"r_oh{k}", [P, NT, E]) for k in range(2)]
    r_tmp = place(cur, "r_tmp", [P, NT, E])
    r_cnt = place(cur, "r_cnt", [P, NT, E])
    r_rank = place(cur, "r_rank", [P, NT, E])
    r_tok = [place(cur, f"r_tok{k}", [P, NT, 3, E], BF16) for k in range(2)]
    r_seq = place(cur, "r_seq", [P, 2, B, E])
    r_top = place(cur, "r_top", [P, 12, NT])
    pos_oh = place(cur, "pos_oh", [P, NPOS, CAP], BF16)
    assert cur[0] <= shared

    cur = [region]
    raw_gu, raw_d, w_hi, w_lo, wd_hi, wd_lo, ex_xhi, ex_xlo, eo, xg = ([None, None] for _ in range(10))
    raw_gu[0] = place(cur, "raw_gu0", [P, 2, C, I])
    raw_d[0] = place(cur, "raw_d0", [P, M, D])
    w_hi[0] = place(cur, "w_hi0", [P, 2, C, I], R32)
    w_lo[0] = place(cur, "w_lo0", [P, 2, C, I], R32)
    xg[0] = place(cur, "xg0", [P, HALF, D])
    assert cur[0] <= route
    cur = [route]
    xg[1] = place(cur, "xg1", [P, HALF, D])
    wd_hi[0] = place(cur, "wd_hi0", [P, M, D], R32)
    wd_lo[0] = place(cur, "wd_lo0", [P, M, D], R32)
    assert cur[0] <= shared
    cur = [shared]
    raw_gu[1] = place(cur, "raw_gu1", [P, 2, C, I])
    raw_d[1] = place(cur, "raw_d1", [P, M, D])
    w_hi[1] = place(cur, "w_hi1", [P, 2, C, I], R32)
    w_lo[1] = place(cur, "w_lo1", [P, 2, C, I], R32)
    wd_hi[1] = place(cur, "wd_hi1", [P, M, D], R32)
    wd_lo[1] = place(cur, "wd_lo1", [P, M, D], R32)
    ex_xhi[0] = place(cur, "ex_xhi0", [P, C, CAP], R32)
    ex_xlo[0] = place(cur, "ex_xlo0", [P, C, CAP], R32)
    assert cur[0] <= sd_at
    cur = [sd_at]
    ex_xhi[1] = place(cur, "ex_xhi1", [P, C, CAP], R32)
    ex_xlo[1] = place(cur, "ex_xlo1", [P, C, CAP], R32)
    for q in range(2):
        eo[q] = place(cur, f"eo{q}", [P, HALF, D])
    ex_hhi = place(cur, "ex_hhi", [P, M, CAP], R32)
    ex_hlo = place(cur, "ex_hlo", [P, M, CAP], R32)
    ex_silu = place(cur, "ex_silu", [P, 2, CAP])
    ex_hid = place(cur, "ex_hid", [P, 2, CAP])
    cur = [region]
    got = place(cur, "got", [P, 2, J, 2, D])

    A_WT, A_XT, A_S, A_RS, A_WSTEP, A_QX, A_QW, A_H, A_UNITS = 0, 1, 2, 3, 4, 5, 7, 9, 13
    B_T, B_S, B_QA, B_WSTEP, B_QW, B_Y, B_X2T, B_LG, B_LGT, B_UNITS = 0, 1, 2, 3, 4, 5, 9, 13, 14, 15
    LINKS_A, LINKS_B = 9, 11
    RING = 3

    with ExitStack() as ctx:
        def sem(name):
            return ctx.enter_context(nc.semaphore(name))

        ps_a = ctx.enter_context(nc.psum_tensor("ps_a", [P, 2, BANK], F32))
        ps_gu = ctx.enter_context(nc.psum_tensor("ps_gu", [P, 2, BANK], F32))
        ps_d = ctx.enter_context(nc.psum_tensor("ps_d", [P, 4, BANK], F32))
        ps_xt = ps_a[:, :, :].rearrange("p u (c n) -> p (u c) n", n=CAP)

        x0_in, x_in, w1_in, w2_in, gates_in, router_in = (sem(n) for n in ("x0_in", "x_in", "w1_in", "w2_in", "gates_in", "router_in"))
        sgu_in, sd_in = sem("sgu_in"), sem("sd_in")
        x2n_out = sem("x2n_out")
        const_ready, masks_ready, tanh_done = sem("const_ready"), sem("masks_ready"), sem("tanh_done")
        router_t, router_hi, router_lo = sem("router_t"), sem("router_hi"), sem("router_lo")
        sgu_hi, sgu_lo, sdn_hi, sdn_lo = sem("sgu_hi"), sem("sgu_lo"), sem("sdn_hi"), sem("sdn_lo")
        full, free = [sem("full_a"), sem("full_b")], [sem("free_a"), sem("free_b")]
        chain, var_done, rstd_done, ratio_done, root_done, pm_done = (
            [sem(f"{n}_{layer}") for layer in "ab"]
            for n in ("chain", "var_done", "rstd_done", "ratio_done", "root_done", "pm_done"))
        smooth_diag, step_diag, ws_done, x_steps, w_steps, x_scaled, w_scaled, qx_done, qw_done = (
            [sem(f"{n}_{layer}") for layer in "ab"]
            for n in ("smooth_diag", "step_diag", "ws_done", "x_steps", "w_steps", "x_scaled", "w_scaled",
                      "qx_done", "qw_done"))
        xn_done, pmx_done, silu_done, gated_done = sem("xn_done"), sem("pmx_done"), sem("silu_done"), sem("gated_done")
        x2n_done, xt_hi_done, logits_staged = sem("x2n_done"), sem("xt_hi_done"), sem("logits_staged")
        sh_gu, sh_sg, sh_h, sh_hi, sh_lo, sh_ring, sh_sum = (
            sem(n) for n in ("sh_gu", "sh_sg", "sh_h", "sh_hi", "sh_lo", "sh_ring", "sh_sum"))
        rt_key = sem("rt_key")
        rt, r_exp_done, seq_done, rank_done = sem("rt"), sem("r_exp_done"), sem("seq_done"), sem("rank_done")
        pos_done, table_mm, idx_ready, routed = (
            sem("pos_done"), sem("table_mm"), sem("idx_ready"), sem("routed"))
        raw_in = [sem("raw_in0"), sem("raw_in1")]
        xg_in = [sem("xg_in0"), sem("xg_in1")]
        eo_out = [sem("eo_out0"), sem("eo_out1")]
        col_done, ex_xt, ex_xh, ex_x = sem("col_done"), sem("ex_xt"), sem("ex_xh"), sem("ex_x")
        ex_whi, ex_wlo, ex_wdhi, ex_wdlo = sem("ex_whi"), sem("ex_wlo"), sem("ex_wdhi"), sem("ex_wdlo")
        ex_gu, ex_sg, ex_h, ex_hi, ex_lo, ex_d, ex_eo = (
            sem(n) for n in ("ex_gu", "ex_sg", "ex_h", "ex_hi", "ex_lo", "ex_d", "ex_eo"))
        cols_staged = sem("cols_staged")
        slot_cols, got_in, sum_half, summed, out_done = (
            sem("slot_cols"), [[sem(f"got_in{k}_{half}") for half in "ab"] for k in range(2)], sem("sum_half"), sem("summed"), sem("out_done"))

        block = ctx.enter_context(nc.Block())

        LA, LB = 0, 1
        COUNT = (A_UNITS, B_UNITS)

        SPARE = ((ps_d[:, 0, :], ps_d[:, 1, :], ps_d[:, 2, :]), (ps_d[:, 3, :], ps_gu[:, 0, :], ps_gu[:, 1, :]))

        def bank(layer, n=0, wide=False):
            return SPARE[layer][n - 1] if wide and n else ps_a[:, layer, :]

        def unit(layer, b, u):
            return COUNT[layer] * b + u + 1

        @block.sync
        def _(sp):
            def load_w1(b):
                sp.dma_start(w1[:], guw_v[b]).then_inc(w1_in, 16)

            def load_w2(b):
                sp.dma_start(w2[:], dw_v[b]).then_inc(w2_in, 16)

            def load_raw(e, q):
                sp.dma_start(raw_gu[q][:, 0], wg_v[e]).then_inc(raw_in[q], 16)
                sp.dma_start(raw_gu[q][:, 1], wu_v[e]).then_inc(raw_in[q], 16)
                sp.dma_start(raw_d[q][:, 0:M - 1, :],
                             w_down[e, 0:(M - 1) * P, :].rearrange("(m p) d -> p m d", p=P)).then_inc(raw_in[q], 16)
                sp.dma_start(raw_d[q][0:ROWS[M - 1], M - 1, :], w_down[e, (M - 1) * P:I, :]).then_inc(raw_in[q], 16)

            def store_x2n(b):
                sp.wait_ge(x2n_done, b + 1)
                sp.dma_start(x2n_v[b], y[:]).then_inc(x2n_out, 16)

            def store_eo(e, q):
                sp.wait_ge(ex_eo, e + 1)
                sp.dma_start(eo_v[e], eo[q][:]).then_inc(eo_out[q], 16)

            sp.dma_start(x2[:, 0], x_v[0]).then_inc(x0_in, 16)
            load_w1(0)
            sp.dma_start(y[0:E, 0, :], gate_w).then_inc(router_in, 16)
            sp.dma_start(tg[:, 0:1], g_x.rearrange("(a n) -> a n", a=1).broadcast_to((P, 1))).then_inc(gates_in, 16)
            sp.dma_start(tg[:, 1:2], g_f.rearrange("(a n) -> a n", a=1).broadcast_to((P, 1))).then_inc(gates_in, 16)
            load_w2(0)
            sp.dma_start(x2[:, 1:B], x_v[1:B].rearrange("b p j d -> p b j d")).then_inc(x_in, 16)
            whole, rest = slice(0, MFULL * P), slice(MFULL * P, IS)
            for n, (src, part, at) in enumerate(((sg_v, whole, 0), (su_v, whole, MFULL * P),
                                                 (sg_v, rest, 2 * MFULL * P), (su_v, rest, 2 * MFULL * P + SREST))):
                width = part.stop - part.start
                sp.dma_start(raw_sgu[:, :, at:at + width], src[:, :, part]).then_inc(sgu_in, 16)
            sp.dma_start(raw_sd[:, 0:MFULL, :],
                         s_down[0:MFULL * P, :].rearrange("(m p) d -> p m d", p=P)).then_inc(sd_in, 16)
            sp.dma_start(raw_sd[0:SREST, MFULL, :], s_down[MFULL * P:IS, :]).then_inc(sd_in, 16)
            sp.wait_ge(qw_done[LA], 1)
            load_w1(1)
            with sp.Fori(1, B - 1) as r:
                sp.wait_ge(qw_done[LB], r)
                load_w2(r)
                sp.wait_ge(qw_done[LA], r + 1)
                load_w1(r + 1)
                store_x2n(r - 1)
            sp.wait_ge(qw_done[LB], B - 1)
            load_w2(B - 1)
            store_x2n(B - 2)
            sp.wait_ge(gated_done, B)
            load_raw(0, 0)
            store_x2n(B - 1)
            sp.wait_ge(sh_gu, MS * B)
            load_raw(1, 1)

            def step(e, q):
                sp.wait_ge(ex_whi, e + 1)
                sp.wait_ge(ex_wlo, e + 1)
                sp.wait_ge(ex_wdhi, e + 1)
                sp.wait_ge(ex_wdlo, e + 1)
                load_raw(e + 2, q)

            step(0, 0)
            with sp.Fori(0, E // 2 - 2) as r:
                step(2 * r + 1, 1)
                store_eo(2 * r, 0)
                step(2 * r + 2, 0)
                store_eo(2 * r + 1, 1)
            step(E - 3, 1)
            for e in range(E - 4, E):
                store_eo(e, e % 2)
            sp.wait_ge(eo_out[0], 16 * (E // 2))
            sp.wait_ge(eo_out[1], 16 * (E // 2))
            with sp.Fori(0, B) as b:
                for half in range(2):
                    j = slice(half * J // 2, (half + 1) * J // 2)
                    sp.wait_ge(summed, 2 * b + half + 1)
                    sp.dma_start(out_v[b][:, j], x2[:, b, j]).then_inc(out_done, 16)
            sp.wait_ge(out_done, 16 * 2 * B)

        @block.gpsimd
        def _(pool):
            pool.memset(ident[:], 0.0).then_inc(const_ready, 1)
            pool.memset(ones[:], 1.0).then_inc(const_ready, 1)
            pool.memset(powers[:, 0, :], 0.5).then_inc(const_ready, 1)
            pool.memset(powers[:, 1, :], -0.5).then_inc(const_ready, 1)
            pool.memset(ln_eps[:], LN_EPS).then_inc(const_ready, 1)
            pool.iota(slot_no[:], [[1, CAP]], base=0, channel_multiplier=0,
                      allow_small_or_imprecise_dtypes=True).then_inc(const_ready, 1)
            pool.iota(rev_e[:], [[-1, E]], base=E, channel_multiplier=0,
                      allow_small_or_imprecise_dtypes=True).then_inc(const_ready, 1)
            for n, (pattern, by_p) in enumerate((([[0, B], [0, J]], J), ([[0, B], [1, J]], 0), ([[T, B], [0, J]], 0))):
                pool.iota(tok_parts[:, n, :], pattern, base=0, channel_multiplier=by_p,
                          allow_small_or_imprecise_dtypes=True).then_inc(const_ready, 1)
            pool.wait_ge(const_ready, 10)
            pool.affine_select(out=ident[:], in_=ident[:], compare_op=ALU.not_equal, fill=1.0, base=0,
                               pattern=[[-1, P]], channel_multiplier=1).then_inc(masks_ready, 1)
            pool.affine_select(out=before[:], in_=ones[:], compare_op=ALU.is_gt, fill=0.0, base=0,
                               pattern=[[1, P]], channel_multiplier=-1).then_inc(masks_ready, 1)
            pool.wait_ge(masks_ready, 2)
            pool.tensor_copy(ident_b[:], ident[:]).then_inc(masks_ready, 1)

            def norm_scale(layer, b):
                sm, done = small[layer], rstd_done[layer]
                pool.wait_ge(var_done[layer], b + 1)
                pool.tensor_tensor(sm["var_eps"][:], mv[layer][:, :, 1], ln_eps[:], ALU.add).then_inc(done, 1)
                pool.wait_ge(done, 2 * b + 1)
                pool.tensor_tensor(sm["rstd"][:], sm["var_eps"][:], powers[:, 1, :], ALU.pow).then_inc(done, 1)

            def root(layer, b, width):
                sm = small[layer]
                pool.wait_ge(ratio_done[layer], b + 1)
                pool.tensor_tensor(sm["root"][:, 0:width], sm["ratio"][:, 0:width], powers[:, 0, 0:width],
                                   ALU.pow).then_inc(root_done[layer], 1)

            def smooth_weights(layer, b, w, row, width, u):
                pool.wait_ge(free[layer], unit(layer, b, u))
                pool.tensor_tensor(w[:], w[:], row[:].unsqueeze(1).broadcast_to((P, J, width)),
                                   ALU.mult).then_inc(ws_done[layer], 1)

            def split_shared(c0, c1):
                pool.wait_ge(sgu_hi, 1)
                pool.tensor_tensor(sw_lo[:, c0:c1, :], raw_sgu[:, c0:c1, :], sw_hi[:, c0:c1, :].bitcast(F32),
                                   ALU.subtract).then_inc(sgu_lo, 1)

            def split_shared_down():
                pool.wait_ge(sdn_hi, 1)
                pool.tensor_tensor(sd_lo[:, 0:MFULL, :], raw_sd[:, 0:MFULL, :], sd_hi[:, 0:MFULL, :].bitcast(F32),
                                   ALU.subtract)
                pool.tensor_tensor(sd_lo[0:SREST, MFULL, :], raw_sd[0:SREST, MFULL, :],
                                   sd_hi[0:SREST, MFULL, :].bitcast(F32), ALU.subtract).then_inc(sdn_lo, 1)

            def iteration(a, b, split_here=False):
                if a is not None:
                    norm_scale(LA, a)
                if b is not None:
                    root(LB, b, C2)
                    smooth_weights(LB, b, w2, row_s_b[:, 0:I2], I2, B_S)
                if a is not None:
                    root(LA, a, C)
                    smooth_weights(LA, a, w1, row_s_a, D, A_S)
                if split_here:
                    split_shared(0, C // 2)
                    split_shared(C // 2, C)
                if b is not None:
                    norm_scale(LB, b)

            iteration(0, None)
            iteration(1, 0, split_here=True)
            split_shared_down()
            with pool.Fori(2, B) as r:
                iteration(r, r - 1)
            iteration(None, B - 1)

            def gather(e, q):
                pool.tensor_copy(idx_col[:, q, :], idx[:, :, e]).then_inc(col_done, 1)
                pool.wait_ge(col_done, e + 1)
                pool.sem_inc(cols_staged, 1)
                for h in range(HALF):
                    pool.indirect_dma_start(xg[q][:, h, :], None, x2n_dram,
                                            bass.IndirectOffsetOnAxis(idx_col[:, q, h:h + 1], 0)).then_inc(xg_in[q], 16)

            def split(e, q):
                pool.wait_ge(ex_whi, e + 1)
                pool.tensor_tensor(w_lo[q][:], raw_gu[q][:], w_hi[q][:].bitcast(F32), ALU.subtract).then_inc(ex_wlo, 1)

            pool.wait_ge(x2n_out, 16 * B)
            pool.wait_ge(free[LB], unit(LB, B - 1, B_LGT))
            split(0, 0)
            pool.wait_ge(idx_ready, 1)
            gather(0, 0)
            pool.wait_ge(routed, 1)
            gather(1, 1)

            def step(e, q):
                split(e + 1, 1 - q)
                pool.wait_ge(ex_xt, e + 1)
                gather(e + 2, q)

            step(0, 0)
            with pool.Fori(0, E // 2 - 2) as r:
                step(2 * r + 1, 1)
                step(2 * r + 2, 0)
            step(E - 3, 1)
            split(E - 1, 1)

            pool.wait_ge(eo_out[0], 16 * (E // 2))
            pool.wait_ge(eo_out[1], 16 * (E // 2))

            def gather_rows(b, k):
                pool.tensor_copy(slot_col[:, k].rearrange("p j n -> p n j"),
                                 slots[:].rearrange("p n (b j) -> p b n j", j=J)[:, b]).then_inc(slot_cols, 1)
                pool.wait_ge(slot_cols, b + 1)
                pool.sem_inc(cols_staged, 1)
                for j in range(J):
                    for n in range(2):
                        pool.indirect_dma_start(got[:, k, j, n, :], None, eo_dram,
                                                bass.IndirectOffsetOnAxis(slot_col[:, k, j, n:n + 1], 0)
                                                ).then_inc(got_in[k][j // 2], 16)

            gather_rows(0, 0)
            gather_rows(1, 1)
            with pool.Fori(1, B // 2) as r:
                for k in range(2):
                    pool.wait_ge(summed, 2 * (2 * r + k - 1))
                    gather_rows(2 * r + k, k)

        @block.scalar
        def _(act):
            act.wait_ge(gates_in, 32)
            act.activation(tg[:], tg[:], ACT.Tanh).then_inc(tanh_done, 1)

            def split_shared():
                act.wait_ge(sgu_in, 64)
                act.activation(sw_hi[:], raw_sgu[:], ACT.Copy).then_inc(sgu_hi, 1)

            def split_shared_down():
                act.wait_ge(sd_in, 32)
                act.activation(sd_hi[:, 0:MFULL, :], raw_sd[:, 0:MFULL, :], ACT.Copy)
                act.activation(sd_hi[0:SREST, MFULL, :], raw_sd[0:SREST, MFULL, :], ACT.Copy).then_inc(sdn_hi, 1)

            def copy_row(layer, b, u, dst, scale=1.0):
                act.wait_ge(full[layer], unit(layer, b, u))
                act.activation(dst[:], bank(layer), ACT.Copy, scale=scale).then_inc(free[layer], 1)

            def quantise(b, src, inv, dst, steps, scaled, done):
                act.wait_ge(steps, b + 1)
                for j in range(J):
                    last = act.activation(src[:, j, :], src[:, j, :], ACT.Copy, bias=MAGIC, scale=inv[:, j:j + 1])
                last.then_inc(scaled, 1)
                rounded(b, src, dst, scaled, done)

            def rounded(b, src, dst, scaled, done):
                act.wait_ge(scaled, b + 1)
                act.activation(dst[:], src[:], ACT.Copy, bias=-MAGIC).then_inc(done, 1)

            def integers(layer, b, u0, u, dst, wide=False, n0=0):
                act.wait_ge(full[layer], unit(layer, b, u0 + u))
                src = bank(layer, n0 + u, wide).bitcast(BF16)
                act.activation(dst[:, 2 * u:2 * u + 2, :], src.rearrange("p (c t) -> p c t", c=2),
                               ACT.Copy).then_inc(free[layer], 1)

            def layer_silu(a):
                act.wait_ge(free[LA], unit(LA, a, A_H + J - 1))
                act.activation(gated[:], xn[:, :, 0:I2], ACT.Silu).then_inc(silu_done, 1)

            def x_hi(b, wide):
                for c in range(C):
                    act.wait_ge(full[LB], unit(LB, b, B_X2T + c))
                    act.activation(xt_hi[:, c, :], bank(LB, c, wide), ACT.Copy).then_inc(xt_hi_done, 1)

            def logits(b):
                act.wait_ge(full[LB], unit(LB, b, B_LG))
                act.activation(diag_b[0:E, :], bank(LB)[0:E, :], ACT.Copy).then_inc(free[LB], 1)

            def token_logits(b):
                act.wait_ge(full[LB], unit(LB, b, B_LGT))
                act.activation(lg[:].rearrange("p (b j) e -> p b (j e)", j=J)[:, b], bank(LB)[:, 0:J * E],
                               ACT.Copy).then_inc(free[LB], 1)

            def sh(f, m):
                n = MS * f + m
                k = P if m < MFULL else SREST
                act.wait_ge(sh_gu, n + 1)
                if m == MFULL:
                    act.wait_ge(sh_lo, n)
                    act.activation(sh_hid[0:SREST, 1 - m % 2, :], ps_gu[SREST:P, 0, :], ACT.Copy)
                act.activation(sh_hid[0:k, m % 2, :], ps_gu[0:k, 0, :], ACT.Silu).then_inc(sh_sg, 1)
                act.wait_ge(sh_h, n + 1)
                act.wait_ge(sh_ring, n + 1)
                act.activation(sh_hhi[0:k, m % RING, :], sh_hid[0:k, m % 2, :], ACT.Copy).then_inc(sh_hi, 1)

            def iteration(a, b, f):
                def sh_chunk(m):
                    if f is not None:
                        sh(f, m)

                sh_chunk(0)
                sh_chunk(1)
                if b is not None:
                    copy_row(LB, b, B_S, row_s_b)
                    quantise(b, gated, small[LB]["x_inv"], ar, x_steps[LB], x_scaled[LB], qx_done[LB])
                sh_chunk(2)
                if a is not None:
                    copy_row(LA, a, A_S, row_s_a)
                if b is not None:
                    integers(LB, b, B_QA, 0, q_a)
                    quantise(b, w2, small[LB]["w_inv"], wr2, w_steps[LB], w_scaled[LB], qw_done[LB])
                    copy_row(LB, b, B_WSTEP, row_w_b, scale=tg[:, 0:1])
                    integers(LB, b, B_QW, 0, q_w2)
                sh_chunk(3)
                if a is not None:
                    quantise(a, xn, small[LA]["x_inv"], xr, x_steps[LA], x_scaled[LA], qx_done[LA])
                    copy_row(LA, a, A_WSTEP, row_w_a)
                    integers(LA, a, A_QX, 0, q_x, f is None)
                    rounded(a, w1, wr, w_scaled[LA], qw_done[LA])
                    integers(LA, a, A_QX, 1, q_x, f is None)
                sh_chunk(4)
                if a is not None:
                    integers(LA, a, A_QW, 0, q_w, f is None, 2)
                    integers(LA, a, A_QW, 1, q_w, f is None, 2)
                sh_chunk(5)
                if b is not None:
                    x_hi(b, f is None)
                if a is not None:
                    layer_silu(a)
                if b is not None:
                    logits(b)
                    token_logits(b)

            act.wait_ge(tanh_done, 1)
            iteration(0, None, None)
            act.wait_ge(router_t, 1)
            act.activation(gate_hi[:], ps_gu[:, 0, 0:C * E].rearrange("p (c e) -> p c e", c=C),
                           ACT.Copy).then_inc(router_hi, 1)
            split_shared()
            split_shared_down()
            iteration(1, 0, None)
            with act.Fori(2, B) as r:
                iteration(r, r - 1, r - 2)
            iteration(None, B - 1, B - 2)

            def weights_gu(e, k, q):
                act.wait_ge(raw_in[q], 64 * k + 64)
                act.activation(w_hi[q][:], raw_gu[q][:], ACT.Copy).then_inc(ex_whi, 1)

            def weights_d(e, q):
                act.activation(wd_hi[q][:, 0:M - 1, :], raw_d[q][:, 0:M - 1, :], ACT.Copy)
                act.activation(wd_hi[q][0:ROWS[M - 1], M - 1, :], raw_d[q][0:ROWS[M - 1], M - 1, :],
                               ACT.Copy).then_inc(ex_wdhi, 1)

            def tokens(e, q):
                act.wait_ge(ex_xt, e + 1)
                act.activation(ex_xhi[q][:], ps_xt, ACT.Copy).then_inc(ex_xh, 1)

            def hidden(e, q, m, first):
                n, k = M * e + m, ROWS[m]
                if first and m == 0:
                    act.wait_ge(sh_sum, B)
                act.wait_ge(ex_gu, n + 1)
                act.activation(ex_silu[0:k, (q + m) % 2, :], ps_gu[0:k, (q + m) % 2, 0:CAP], ACT.Silu).then_inc(ex_sg, 1)
                act.wait_ge(ex_h, n + 1)
                if not first:
                    act.wait_ge(ex_d, n - M + 1)
                act.activation(ex_hhi[0:k, m, :], ex_hid[0:k, (q + m) % 2, :], ACT.Copy).then_inc(ex_hi, 1)

            def rows_out(e, k, q):
                act.wait_ge(ex_d, M * e + M)
                if k is not None:
                    act.wait_ge(eo_out[q], 16 * k)
                act.activation(eo[q][:], ps_d[:, 2 * q:2 * q + 2, :], ACT.Copy).then_inc(ex_eo, 1)

            def step(e, k, q, first=False, last=False, evict=True):
                if not last:
                    weights_gu(e + 1, k + q, 1 - q)
                hidden(e, q, 0, first)
                if not first:
                    rows_out(e - 1, k - 1 + q if evict else None, 1 - q)
                hidden(e, q, 1, first)
                if not last:
                    tokens(e + 1, 1 - q)
                hidden(e, q, 2, first)
                if not last:
                    weights_d(e + 1, 1 - q)

            act.wait_ge(rt_key, 1)
            act.activation(r_exp[:], r_key[:], ACT.Exp).then_inc(r_exp_done, 1)
            for m in range(MS):
                sh(B - 1, m)
                if m == 1:
                    weights_gu(0, 0, 0)
            tokens(0, 0)
            act.wait_ge(routed, 1)
            weights_d(0, 0)
            step(0, 0, 0, first=True)
            step(1, 0, 1, evict=False)
            step(2, 1, 0, evict=False)
            with act.Fori(1, E // 2 - 1) as r:
                step(2 * r + 1, r, 1)
                step(2 * r + 2, r + 1, 0)
            step(E - 1, E // 2 - 1, 1, last=True)
            rows_out(E - 1, E // 2 - 1, 1)

        @block.vector
        def _(dve):
            links = [0, 0]
            LINKS = (LINKS_A, LINKS_B)

            def link(ins, layer, b):
                links[layer] += 1
                ins.then_inc(chain[layer], 1)
                dve.wait_ge(chain[layer], LINKS[layer] * b + links[layer])

            def partial(src, dst):
                return dve.tensor_reduce(dst, src.rearrange("p j d -> p d j"), AX.X, ALU.max, apply_absolute_value=True)

            def moments(layer, b, n):
                for j in range(J):
                    last = dve.bn_stats(bn[layer][:, j, :], x2[:, n, j, :])
                link(last, layer, b)
                dve.memset(after_wait[:], 0.0)
                for j in range(J):
                    last = dve.bn_aggr(mv[layer][:, j, :], bn[layer][:, j, :])
                last.then_inc(var_done[layer], 1)

            def normalise(layer, b, dst, done):
                dve.wait_ge(rstd_done[layer], 2 * b + 2)
                for j in range(J):
                    last = dve.tensor_scalar(dst[:, j, :], x2[:, b, j, :], mv[layer][:, j, 0:1],
                                             small[layer]["rstd"][:, j:j + 1], ALU.subtract, ALU.mult)
                last.then_inc(done, 1)

            def largest(layer, b, u, dst, width):
                dve.wait_ge(full[layer], unit(layer, b, u))
                dve.tensor_reduce(dst, bank(layer)[:, 0:width * P].rearrange("p (c q) -> p c q", q=P), AX.X,
                                  ALU.max).then_inc(free[layer], 1)

            def ratio(layer, b, u, w_max, x_max):
                sm, width = small[layer], w_max.shape[1]
                w = sm["recip_w"][:, 0:width]
                dve.wait_ge(free[layer], unit(layer, b, u))
                link(dve.tensor_scalar(w, w_max, Q_EPS, None, ALU.max), layer, b)
                link(dve.reciprocal(w, w), layer, b)
                dve.scalar_tensor_tensor(out=sm["ratio"][:, 0:width], in0=x_max, scalar=Q_EPS, in1=w,
                                         op0=ALU.max, op1=ALU.mult).then_inc(ratio_done[layer], 1)

            def diagonals(layer, diag, src, n):
                for c in range(n):
                    last = dve.tensor_scalar(diag[:, c * P:(c + 1) * P], ident[:], small[layer][src][:, c:c + 1], None,
                                             ALU.mult)
                return last

            def smoothing(layer, b, diag, diag_r, n):
                sm = small[layer]
                dve.wait_ge(root_done[layer], b + 1)
                link(dve.tensor_scalar(sm["smooth"][:, 0:n], sm["root"][:, 0:n], Q_EPS, None, ALU.max), layer, b)
                last = diagonals(layer, diag, "smooth", n)
                if layer == LA:
                    last.then_inc(smooth_diag[layer], 1)
                link(dve.reciprocal(sm["rsmooth"][:, 0:n], sm["smooth"][:, 0:n]), layer, b)
                diagonals(layer, diag_r, "rsmooth", n).then_inc(smooth_diag[layer], 1)

            def step_sizes(layer, b, which, src, done):
                sm = small[layer]
                link(dve.tensor_reduce(sm[which + "_max"][:], src[:], AX.X, ALU.max, apply_absolute_value=True), layer, b)
                link(dve.tensor_scalar(sm[which + "_step"][:], sm[which + "_max"][:], Q_EPS, 1.0 / QMAX,
                                       ALU.max, ALU.mult), layer, b)
                dve.reciprocal(sm[which + "_inv"][:], sm[which + "_step"][:]).then_inc(done, 1)

            def first_activations(a, wide):
                dve.wait_ge(free[LA], unit(LA, a, A_S))
                dve.wait_ge(full[LA], unit(LA, a, A_RS))
                dve.tensor_tensor(xn[:], xn[:], bank(LA, 1, wide).unsqueeze(1).broadcast_to((P, J, D)),
                                  ALU.mult).then_inc(free[LA], 1)
                dve.wait_ge(free[LA], unit(LA, a, A_RS))
                step_sizes(LA, a, "x", xn, x_steps[LA])

            def second_activations(b):
                dve.wait_ge(free[LB], unit(LB, b, B_S))
                link(dve.tensor_tensor(gated[:], gated[:], row_s_b[:, I2:2 * I2].unsqueeze(1).broadcast_to((P, J, I2)),
                                       ALU.mult), LB, b)
                step_sizes(LB, b, "x", gated, x_steps[LB])

            def weight_steps(layer, b, w, diag):
                dve.wait_ge(ws_done[layer], b + 1)
                step_sizes(layer, b, "w", w, w_steps[layer])
                diagonals(layer, diag, "w_step", J).then_inc(step_diag[layer], 1)

            def dequantise(layer, b, u0, j, row, dst, wide):
                dve.wait_ge(full[layer], unit(layer, b, u0 + j))
                dve.scalar_tensor_tensor(out=dst[:, j, :], in0=bank(layer, j, wide),
                                         scalar=small[layer]["x_step"][:, j:j + 1], in1=row[:],
                                         op0=ALU.mult, op1=ALU.mult).then_inc(free[layer], 1)

            def sh(f, m):
                n = MS * f + m
                k = P if m < MFULL else SREST
                dve.wait_ge(sh_sg, n + 1)
                up = ps_gu[:, 1, :] if m < MFULL else sh_hid[0:SREST, 1 - m % 2, :]
                dve.tensor_tensor(sh_hid[0:k, m % 2, :], sh_hid[0:k, m % 2, :], up, ALU.mult).then_inc(sh_h, 1)
                dve.wait_ge(sh_hi, n + 1)
                dve.tensor_tensor(sh_hlo[0:k, m % RING, :], sh_hid[0:k, m % 2, :],
                                  sh_hhi[0:k, m % RING, :].bitcast(F32), ALU.subtract).then_inc(sh_lo, 1)

            def sh_add(f):
                dve.wait_ge(sh_ring, RING + MS * f + MS)
                for j in range(J):
                    last = dve.scalar_tensor_tensor(out=x2[:, f, j, :], in0=ps_d[:, j, :], scalar=tg[:, 1:2],
                                                    in1=x2[:, f, j, :], op0=ALU.mult, op1=ALU.add)
                last.then_inc(sh_sum, 1)

            def iteration(a, b, f):
                links[:] = [0, 0]

                def sh_chunk(m):
                    if f is not None:
                        sh(f, m)

                if b is not None:
                    dve.wait_ge(gated_done, b + 1)
                    partial(gated[:], row_w_b[:, I2:2 * I2]).then_inc(pm_done[LB], 1)
                if a is not None:
                    dve.wait_ge(x0_in if b is None else x_in, 16)
                    dve.memset(after_wait[:], 0.0)
                    moments(LA, a, a)
                if b is not None:
                    w_x = small[LB]["amax_w"]
                    largest(LB, b, B_T, w_x[:], 2 * C2)
                    ratio(LB, b, B_T, w_x[:, 0:C2], w_x[:, C2:2 * C2])
                sh_chunk(0)
                if b is not None:
                    smoothing(LB, b, diag_b, diag_b[:, I2:2 * I2], C2)
                if a is not None:
                    dve.wait_ge(w1_in, 16 * a + 16)
                    partial(w1[:], row_w_a[:]).then_inc(pm_done[LA], 1)
                    normalise(LA, a, xn, xn_done)
                    dve.wait_ge(xn_done, a + 1)
                    partial(xn[:], diag_a[:]).then_inc(pmx_done, 1)
                    largest(LA, a, A_WT, small[LA]["amax_w"][:], C)
                sh_chunk(1)
                if b is not None:
                    second_activations(b)
                if a is not None:
                    largest(LA, a, A_XT, small[LA]["amax_x"][:], C)
                    ratio(LA, a, A_XT, small[LA]["amax_w"][:], small[LA]["amax_x"][:])
                if b is not None:
                    weight_steps(LB, b, w2, diag_b)
                if a is not None:
                    smoothing(LA, a, diag_a, row_w_a, C)
                sh_chunk(2)
                if a is not None:
                    first_activations(a, f is None)
                sh_chunk(3)
                if b is not None:
                    if not (isinstance(b, int) and b == 0):
                        dve.wait_ge(x2n_out, 16 * b)
                    dve.wait_ge(free[LB], unit(LB, b, B_WSTEP))
                    dequantise(LB, b, B_Y, 0, row_w_b, y, f is None)
                if a is not None:
                    weight_steps(LA, a, w1, diag_a)
                if b is not None:
                    dequantise(LB, b, B_Y, 1, row_w_b, y, f is None)
                if a is not None:
                    dve.wait_ge(w_steps[LA], a + 1)
                    for j in range(J):
                        last = dve.tensor_scalar(w1[:, j, :], w1[:, j, :], small[LA]["w_inv"][:, j:j + 1], MAGIC,
                                                 ALU.mult, ALU.add)
                    last.then_inc(w_scaled[LA], 1)
                if b is not None:
                    dequantise(LB, b, B_Y, 2, row_w_b, y, f is None)
                    dequantise(LB, b, B_Y, 3, row_w_b, y, f is None)
                if b is not None:
                    dve.wait_ge(free[LB], unit(LB, b, B_Y + J - 1))
                    link(dve.tensor_tensor(x2[:, b], x2[:, b], y[:], ALU.add), LB, b)
                    dve.memset(after_wait[:], 0.0)
                sh_chunk(4)
                if b is not None:
                    moments(LB, b, b)
                if a is not None:
                    dve.wait_ge(w2_in, 16 * a + 16)
                    partial(w2[:], row_w_b[:, 0:I2])
                if b is not None:
                    normalise(LB, b, y, x2n_done)
                if a is not None:
                    dve.wait_ge(free[LA], unit(LA, a, A_WSTEP))
                    dequantise(LA, a, A_H, 0, row_w_a, xn, f is None)
                sh_chunk(5)
                for c in range(C):
                    if a is not None and c > 0:
                        dequantise(LA, a, A_H, c, row_w_a, xn, f is None)
                    if b is not None:
                        dve.wait_ge(xt_hi_done, C * b + c + 1)
                        dve.tensor_tensor(xt_lo[:, c, :], bank(LB, c, f is None), xt_hi[:, c, :].bitcast(F32),
                                          ALU.subtract).then_inc(free[LB], 1)
                if a is not None:
                    dve.wait_ge(silu_done, a + 1)
                    dve.tensor_tensor(gated[:], gated[:], xn[:, :, I2:D], ALU.mult).then_inc(gated_done, 1)
                if f is not None:
                    sh_add(f)
                assert links[LA] in (0, LINKS_A) and links[LB] in (0, LINKS_B), links

            iteration(0, None, None)
            dve.wait_ge(router_hi, 1)
            dve.tensor_tensor(gate_lo[:], ps_gu[:, 0, 0:C * E].rearrange("p (c e) -> p c e", c=C),
                              gate_hi[:].bitcast(F32), ALU.subtract).then_inc(router_lo, 1)
            iteration(1, 0, None)
            with dve.Fori(2, B) as r:
                iteration(r, r - 1, r - 2)
            iteration(None, B - 1, B - 2)

            steps = [0]

            def then(ins):
                steps[0] += 1
                ins.then_inc(rt, 1)
                dve.wait_ge(rt, steps[0])

            def per_tile(ap):
                return ap.unsqueeze(2).broadcast_to((P, NT, E))

            last_f = B - 1
            rev = rev_e[:].unsqueeze(1).broadcast_to((P, NT, E))
            T_MAX, T_SUM, T_E, T_W, T_POS = 0, 1, 2, 4, 6

            def top(k):
                return r_top[:, k, :]

            dve.wait_ge(free[LB], unit(LB, B - 1, B_LGT))
            then(dve.tensor_reduce(top(T_MAX), lg[:], AX.X, ALU.max))
            then(dve.tensor_tensor(r_key[:], lg[:], per_tile(top(T_MAX)), ALU.subtract))
            then(dve.tensor_scalar(r_key[:], r_key[:], EXP_MIN, None, ALU.max))
            dve.tensor_copy(r_tmp[:], r_key[:]).then_inc(rt_key, 1)
            dve.wait_ge(rt_key, 1)
            for k in range(2):
                then(dve.tensor_reduce(top(T_MAX), r_tmp[:], AX.X, ALU.max))
                then(dve.tensor_tensor(r_cnt[:], r_tmp[:], per_tile(top(T_MAX)), ALU.is_equal))
                then(dve.tensor_tensor(r_cnt[:], r_cnt[:], rev, ALU.mult))
                then(dve.tensor_reduce(top(T_E + k), r_cnt[:], AX.X, ALU.max))
                then(dve.tensor_tensor(r_oh[k][:], rev, per_tile(top(T_E + k)), ALU.is_equal))
                if k == 0:
                    then(dve.scalar_tensor_tensor(out=r_tmp[:], in0=r_oh[0][:], scalar=4 * EXP_MIN, in1=r_tmp[:],
                                                  op0=ALU.mult, op1=ALU.add))
                    sh(last_f, 0)
            then(dve.tensor_tensor(r_cnt[:], r_oh[0][:], r_oh[1][:], ALU.add))
            then(dve.tensor_reduce(r_seq[:, 0], r_cnt[:].rearrange("p (b j) e -> p b e j", j=J), AX.X, ALU.add))
            then(dve.memset(r_seq[:, 1, 0, :], 0.0))
            for b in range(1, B):
                last = dve.tensor_tensor(r_seq[:, 1, b, :], r_seq[:, 1, b - 1, :], r_seq[:, 0, b - 1, :], ALU.add)
                then(last) if b < B - 1 else last.then_inc(seq_done, 1)
            sh(last_f, 1)
            dve.wait_ge(rank_done, 1)
            cnt = r_cnt[:].rearrange("p (b j) e -> p b j e", j=J)
            rank = r_rank[:].rearrange("p (b j) e -> p b j e", j=J)
            then(dve.tensor_copy(rank[:, :, 0, :], ps_a[:, 0, 0:B * E].rearrange("p (b e) -> p b e", e=E)))
            for j in range(1, J):
                then(dve.tensor_tensor(rank[:, :, j, :], rank[:, :, j - 1, :], cnt[:, :, j - 1, :], ALU.add))
            for k in range(2):
                then(dve.tensor_tensor(r_tmp[:], r_oh[k][:], r_rank[:], ALU.mult))
                then(dve.tensor_reduce(top(T_POS + k), r_tmp[:], AX.X, ALU.add))
                for n in range(3):
                    then(dve.tensor_tensor(r_tok[k][:, :, n, :], r_oh[k][:], per_tile(tok_parts[:, n, :]), ALU.mult))
            for n in range(2 * NT):
                i, k = divmod(n, 2)
                if n >= NPOS:
                    dve.wait_ge(table_mm, n - NPOS + 1)
                dve.tensor_scalar(pos_oh[:, n % NPOS, :], slot_no[:], top(T_POS + k)[:, i:i + 1], None,
                                  ALU.is_equal).then_inc(pos_done, 1)
                if n == NPOS - 1:
                    sh(last_f, 2)
            sh(last_f, 3)
            dve.wait_ge(table_mm, 2 * NT)
            for h in range(HALF):
                last = dve.tensor_reduce(r_tmp[:, h, :], ps_a[:, h, 0:3 * E].rearrange("p (n e) -> p e n", e=E), AX.X, ALU.add)
            then(last)
            dve.tensor_copy(idx[:], r_tmp[:, 0:HALF, :]).then_inc(idx_ready, 1)
            sh(last_f, 4)
            for k in range(2):
                then(dve.tensor_scalar(top(T_POS + k), top(T_POS + k), float(CAP - 1), float(E * CAP), ALU.min, ALU.add))
                then(dve.scalar_tensor_tensor(out=top(T_POS + k), in0=top(T_E + k), scalar=-float(CAP),
                                              in1=top(T_POS + k), op0=ALU.mult, op1=ALU.add))
                then(dve.tensor_copy(slots[:, k, :], top(T_POS + k)))
            dve.wait_ge(r_exp_done, 1)
            then(dve.tensor_reduce(top(T_SUM), r_exp[:], AX.X, ALU.add))
            then(dve.reciprocal(top(T_SUM), top(T_SUM)))
            for k in range(2):
                then(dve.tensor_tensor(r_tmp[:], r_exp[:], r_oh[k][:], ALU.mult))
                then(dve.tensor_reduce(top(T_W + k), r_tmp[:], AX.X, ALU.add))
                last = dve.scalar_tensor_tensor(out=wts[:, k, :], in0=top(T_W + k), scalar=tg[:, 1:2], in1=top(T_SUM),
                                                op0=ALU.mult, op1=ALU.mult)
            last.then_inc(routed, 1)
            sh(last_f, 5)

            def weights_d(e, q):
                dve.wait_ge(ex_wdhi, e + 1)
                dve.tensor_tensor(wd_lo[q][:, 0:M - 1, :], raw_d[q][:, 0:M - 1, :], wd_hi[q][:, 0:M - 1, :].bitcast(F32),
                                  ALU.subtract)
                k = ROWS[M - 1]
                dve.tensor_tensor(wd_lo[q][0:k, M - 1, :], raw_d[q][0:k, M - 1, :], wd_hi[q][0:k, M - 1, :].bitcast(F32),
                                  ALU.subtract).then_inc(ex_wdlo, 1)

            def tokens(e, q):
                dve.wait_ge(ex_xh, e + 1)
                dve.tensor_tensor(ex_xlo[q][:], ps_xt, ex_xhi[q][:].bitcast(F32), ALU.subtract).then_inc(ex_x, 1)

            def hidden(e, q, m):
                n, k = M * e + m, ROWS[m]
                dve.wait_ge(ex_sg, n + 1)
                dve.tensor_tensor(ex_hid[0:k, (q + m) % 2, :], ex_silu[0:k, (q + m) % 2, :],
                                  ps_gu[0:k, (q + m) % 2, CAP:2 * CAP], ALU.mult).then_inc(ex_h, 1)
                dve.wait_ge(ex_hi, n + 1)
                dve.tensor_tensor(ex_hlo[0:k, m, :], ex_hid[0:k, (q + m) % 2, :], ex_hhi[0:k, m, :].bitcast(F32),
                                  ALU.subtract).then_inc(ex_lo, 1)

            def step(e, q, last=False):
                hidden(e, q, 0)
                hidden(e, q, 1)
                if not last:
                    tokens(e + 1, 1 - q)
                hidden(e, q, 2)
                if not last:
                    weights_d(e + 1, 1 - q)

            tokens(0, 0)
            sh_add(last_f)
            weights_d(0, 0)
            step(0, 0)
            with dve.Fori(0, E // 2 - 1) as r:
                step(2 * r + 1, 1)
                step(2 * r + 2, 0)
            step(E - 1, 1, last=True)

            def add_rows(b, r, k, half):
                dve.wait_ge(got_in[k][half], 16 * J * (r + 1))
                x2_b, w_b = x2[:, b], wts[:].rearrange("p n (b j) -> p b n j", j=J)[:, b]
                tiles = range(half * J // 2, (half + 1) * J // 2)
                for j in tiles:
                    last = dve.scalar_tensor_tensor(out=x2_b[:, j, :], in0=got[:, k, j, 0, :], scalar=w_b[:, 0, j:j + 1],
                                                    in1=x2_b[:, j, :], op0=ALU.mult, op1=ALU.add)
                last.then_inc(sum_half, 1)
                dve.wait_ge(sum_half, 2 * b + half + 1)
                for j in tiles:
                    last = dve.scalar_tensor_tensor(out=x2_b[:, j, :], in0=got[:, k, j, 1, :], scalar=w_b[:, 1, j:j + 1],
                                                    in1=x2_b[:, j, :], op0=ALU.mult, op1=ALU.add)
                last.then_inc(summed, 1)

            with dve.Fori(0, B // 2) as r:
                for k in range(2):
                    for half in range(2):
                        add_rows(2 * r + k, r, k, half)

        @block.tensor
        def _(pe):
            def three(dst, a_hi, a_lo, b_hi, b_lo, start, stop):
                pe.matmul(dst, a_hi, b_hi, start=start, stop=False)
                pe.matmul(dst, a_hi, b_lo, start=False, stop=False)
                return pe.matmul(dst, a_lo, b_hi, start=False, stop=stop)

            pe.wait_ge(masks_ready, 3)

            def empty(layer, b, u, spare=False):
                if spare:
                    return
                if u > 0 or not (isinstance(b, int) and b == 0):
                    pe.wait_ge(free[layer], unit(layer, b, u) - 1)

            def turned_maxima(layer, b, u, sem_, src):
                pe.wait_ge(sem_, b + 1)
                empty(layer, b, u)
                for c in range(C):
                    last = pe.transpose(bank(layer)[:, c * P:(c + 1) * P], src[:, c * P:(c + 1) * P], ident[:])
                last.then_inc(full[layer], 1)

            def turned_integers(layer, b, u0, c0, sem_, src, n=0, wide=False):
                pe.wait_ge(sem_, b + 1)
                out16 = bank(layer, n, wide).bitcast(BF16)
                for c in (c0, c0 + 1):
                    if c % 2 == 0:
                        empty(layer, b, u0 + c // 2, wide and n > 0)
                    for j in range(J):
                        at = (c % 2 * J + j) * P
                        last = pe.transpose(out16[:, at:at + P], src[:, j, c * P:(c + 1) * P], ident_b[:])
                    if c % 2:
                        last.then_inc(full[layer], 1)

            def row(layer, b, u, sem_, count, diag, n=0, wide=False):
                pe.wait_ge(sem_, count)
                empty(layer, b, u, wide and n > 0)
                pe.matmul(bank(layer, n, wide), ones[:], diag[:], start=True, stop=True).then_inc(full[layer], 1)

            def integer_product(layer, b, u0, j, n, qx, qw, wide):
                empty(layer, b, u0 + j, wide and j > 0)
                for c in range(n):
                    last = pe.matmul(bank(layer, j, wide), qx[:, c, j * P:(j + 1) * P], qw[:, c, :], start=(c == 0), stop=(c == n - 1))
                last.then_inc(full[layer], 1)

            def sh_up(f, m, halves=(0, 1)):
                n = MS * f + m
                if halves[0] == 0:
                    if m == 0:
                        pe.wait_ge(free[LB], unit(LB, f, B_X2T + C - 1))
                    else:
                        pe.wait_ge(sh_h, n)
                parts = ((0, m * P), (1, (MFULL + m) * P)) if m < MFULL else ((0, 2 * MFULL * P),)
                for u, at in parts:
                    if u in halves:
                        for c in range(C):
                            last = three(ps_gu[:, u, :], sw_hi[:, c, at:at + P], sw_lo[:, c, at:at + P],
                                         xt_hi[:, c, :], xt_lo[:, c, :], c == 0, c == C - 1)
                if halves[-1] == 1:
                    last.then_inc(sh_gu, 1)

            def sh_down(f, m, tiles=(0, 1, 2, 3)):
                n = MS * f + m
                k = P if m < MFULL else SREST
                if tiles[0] == 0:
                    pe.wait_ge(sh_lo, n + 1)
                for j in tiles:
                    t = slice(j * P, (j + 1) * P)
                    last = three(ps_d[:, j, :], sh_hhi[0:k, m % RING, t], sh_hlo[0:k, m % RING, t],
                                 sd_hi[0:k, m, :], sd_lo[0:k, m, :], m == 0, m == MS - 1)
                if tiles[-1] == J - 1:
                    last.then_inc(sh_ring, 1)

            def iteration(a, b, f):
                def up(*chunk):
                    if f is not None:
                        sh_up(f, *chunk)

                def down(*chunk):
                    if f is not None:
                        sh_down(f, *chunk)

                def first_product(j):
                    if a is not None:
                        integer_product(LA, a, A_H, j, C, q_x, q_w, f is None)

                def second_product(j):
                    if b is not None:
                        integer_product(LB, b, B_Y, j, C2, q_a, q_w2, f is None)

                def turned_tokens(c):
                    if b is not None:
                        empty(LB, b, B_X2T + c, f is None and c > 0)
                        for j in range(J):
                            last = pe.transpose(bank(LB, c, f is None)[:, j * P:(j + 1) * P], y[:, j, c * P:(c + 1) * P], ident[:])
                        last.then_inc(full[LB], 1)

                up(0, (0,))
                if b is not None:
                    turned_maxima(LB, b, B_T, pm_done[LB], row_w_b)
                up(0, (1,))
                up(1)
                if b is not None:
                    row(LB, b, B_S, smooth_diag[LB], b + 1, diag_b)
                if a is not None:
                    turned_maxima(LA, a, A_WT, pm_done[LA], row_w_a)
                down(0)
                if a is not None:
                    turned_maxima(LA, a, A_XT, pmx_done, diag_a)
                up(2)
                down(1, (0, 1))
                if b is not None:
                    turned_integers(LB, b, B_QA, 0, qx_done[LB], ar)
                if a is not None:
                    row(LA, a, A_S, smooth_diag[LA], 2 * a + 1, diag_a)
                down(1, (2, 3))
                if a is not None:
                    row(LA, a, A_RS, smooth_diag[LA], 2 * a + 2, row_w_a, 1, f is None)
                if b is not None:
                    row(LB, b, B_WSTEP, step_diag[LB], b + 1, diag_b)
                up(3, (0,))
                if b is not None:
                    turned_integers(LB, b, B_QW, 0, qw_done[LB], wr2)
                up(3, (1,))
                second_product(0)
                down(2, (0, 1))
                up(4, (0,))
                second_product(1)
                up(4, (1,))
                if a is not None:
                    row(LA, a, A_WSTEP, step_diag[LA], a + 1, diag_a)
                second_product(2)
                if a is not None:
                    turned_integers(LA, a, A_QX, 0, qx_done[LA], xr, 0, f is None)
                down(2, (2, 3))
                second_product(3)
                if a is not None:
                    turned_integers(LA, a, A_QX, 2, qx_done[LA], xr, 1, f is None)
                down(3, (0, 1))
                if a is not None:
                    turned_integers(LA, a, A_QW, 0, qw_done[LA], wr, 2, f is None)
                down(3, (2, 3))
                if a is not None:
                    turned_integers(LA, a, A_QW, 2, qw_done[LA], wr, 3, f is None)
                up(5)
                first_product(0)
                down(4, (0, 1))
                if b is not None:
                    pe.wait_ge(x2n_done, b + 1)
                turned_tokens(0)
                first_product(1)
                down(4, (2, 3))
                turned_tokens(1)
                first_product(2)
                down(5, (0, 1))
                turned_tokens(2)
                first_product(3)
                down(5, (2,))
                turned_tokens(3)
                down(5, (3,))
                if b is not None:
                    empty(LB, b, B_LG)
                    if isinstance(b, int) and b == 0:
                        pe.wait_ge(router_lo, 1)
                    for c in range(C):
                        last = three(bank(LB)[0:E, :], gate_hi[:, c, :], gate_lo[:, c, :], xt_hi[:, c, :], xt_lo[:, c, :],
                                     c == 0, c == C - 1)
                    last.then_inc(full[LB], 1)
                    empty(LB, b, B_LGT)
                    pe.sem_inc(logits_staged, 1)
                    for j in range(J):
                        last = pe.transpose(bank(LB)[:, j * E:(j + 1) * E], diag_b[0:E, j * P:(j + 1) * P], ident[0:E, 0:E])
                    last.then_inc(full[LB], 1)

            pe.sem_inc(sh_ring, RING)
            iteration(0, None, None)
            pe.wait_ge(router_in, 16)
            for c in range(C):
                last = pe.transpose(ps_gu[:, 0, c * E:(c + 1) * E], y[0:E, 0, c * P:(c + 1) * P], ident[0:E, 0:E])
            last.then_inc(router_t, 1)
            iteration(1, 0, None)
            pe.wait_ge(sgu_hi, 1)
            pe.wait_ge(sgu_lo, 2)
            pe.wait_ge(sdn_hi, 1)
            pe.wait_ge(sdn_lo, 1)
            with pe.Fori(2, B) as r:
                iteration(r, r - 1, r - 2)
            iteration(None, B - 1, B - 2)

            f = B - 1
            sh_up(f, 0)
            sh_up(f, 1)
            sh_down(f, 0)
            pe.wait_ge(seq_done, 1)
            pe.matmul(ps_a[:, 0, 0:B * E], before[:], r_seq[:, 0].rearrange("p b e -> p (b e)"), start=True, stop=False)
            pe.matmul(ps_a[:, 0, 0:B * E], ones[:], r_seq[:, 1].rearrange("p b e -> p (b e)"), start=False,
                      stop=True).then_inc(rank_done, 1)
            sh_up(f, 2)
            sh_down(f, 1)

            def table(n0, n1):
                for n in range(n0, n1):
                    i, k = divmod(n, 2)
                    pe.wait_ge(pos_done, n + 1)
                    for h in range(HALF):
                        last = pe.matmul(ps_a[:, h, 0:3 * E], pos_oh[:, n % NPOS, h * P:(h + 1) * P],
                                         r_tok[k][:, i].rearrange("p n e -> p (n e)"),
                                         start=(n == 0), stop=(n == 2 * NT - 1))
                    last.then_inc(table_mm, 1)

            table(0, NPOS)
            sh_up(f, 3)
            sh_down(f, 2)
            table(NPOS, 2 * NT)
            sh_up(f, 4)
            sh_down(f, 3)
            sh_up(f, 5)
            sh_down(f, 4)

            def turn_tokens(e, k, q):
                pe.wait_ge(xg_in[q], 32 * k + 32)
                for c in range(C):
                    for h in range(HALF):
                        last = pe.transpose(ps_xt[:, c, h * P:(h + 1) * P], xg[q][:, h, c * P:(c + 1) * P], ident[:])
                last.then_inc(ex_xt, 1)

            def up(e, q, m, first=False):
                n, k = M * e + m, ROWS[m]
                if m == 0:
                    pe.wait_ge(ex_x, e + 1)
                    pe.wait_ge(ex_whi, e + 1)
                    pe.wait_ge(ex_wlo, e + 1)
                if not first or m == 2:
                    pe.wait_ge(ex_h, n - 1)
                u = (q + m) % 2
                for g in range(2):
                    for c in range(C):
                        i = slice(m * P, m * P + k)
                        last = three(ps_gu[0:k, u, g * CAP:(g + 1) * CAP], w_hi[q][:, g, c, i], w_lo[q][:, g, c, i],
                                     ex_xhi[q][:, c, :], ex_xlo[q][:, c, :], c == 0, c == C - 1)
                last.then_inc(ex_gu, 1)

            def down(e, q, m, evicted=True):
                n, k = M * e + m, ROWS[m]
                pe.wait_ge(ex_lo, n + 1)
                if m == 0:
                    pe.wait_ge(ex_wdlo, e + 1)
                    if not evicted:
                        pe.wait_ge(sh_sum, B)
                    else:
                        pe.wait_ge(ex_eo, e - 1)
                for h in range(HALF):
                    t = slice(h * P, (h + 1) * P)
                    last = three(ps_d[:, 2 * q + h, :], ex_hhi[0:k, m, t], ex_hlo[0:k, m, t],
                                 wd_hi[q][0:k, m, :], wd_lo[q][0:k, m, :], m == 0, m == M - 1)
                last.then_inc(ex_d, 1)

            def step(e, k, q, first=False, last=False, evicted=True):
                up(e, q, 0, first)
                if not first:
                    down(e - 1, 1 - q, 2)
                up(e, q, 1, first)
                down(e, q, 0, evicted)
                if not last:
                    turn_tokens(e + 1, k + q, 1 - q)
                up(e, q, 2, first)
                down(e, q, 1)

            pe.wait_ge(idx_ready, 1)
            turn_tokens(0, 0, 0)
            sh_down(f, 5)
            step(0, 0, 0, first=True, evicted=False)
            step(1, 0, 1, evicted=False)
            step(2, 1, 0)
            with pe.Fori(1, E // 2 - 1) as r:
                step(2 * r + 1, r, 1)
                step(2 * r + 2, r + 1, 0)
            step(E - 1, E // 2 - 1, 1, last=True)
            down(E - 1, 1, 2)


_INS = ['x', 'fside_BxS2xS2_0', 'ctx_1024', 'g_xattn', 'g_ffn', 'L0_ffn_gate_w', 'L0_ffn_w_gate', 'L0_ffn_w_up',
        'L0_ffn_w_down', 'L0_ffn_ws_gate', 'L0_ffn_ws_up', 'L0_ffn_ws_down']


def kernel(**inputs):
    import numpy as _np
    import concourse.bacc as _bacc
    from concourse import mybir as _mybir
    from concourse.bass_utils import run_bass_kernel_spmd as _run

    nc = _bacc.Bacc("TRN2", target_bir_lowering=False, num_devices=1)
    arrays, args = {}, []
    for name in _INS:
        a = _np.ascontiguousarray(inputs[name])
        arrays[f"in_{name}"] = a
        args.append(nc.dram_tensor(f"in_{name}", a.shape, _mybir.dt.from_np(a.dtype), kind="ExternalInput").ap())
    out = nc.dram_tensor("out", inputs["x"].shape, _mybir.dt.float32, kind="ExternalOutput").ap()
    flamingo_block(nc, *args, out)
    r = _run(nc, [arrays], core_ids=[0])
    return r.results[0]["out"]
```
